# Optimizing a Trainium2 kernel written in Bass

```python
import numpy as np
import jax
import jax.numpy as jnp

def _softmax(x, axis=-1):
    return jax.nn.softmax(x, axis=axis)

def _gelu(x):
    return jax.nn.gelu(x, approximate=True)

def _silu(x):
    return jax.nn.silu(x)

def _sigmoid(x):
    return jax.nn.sigmoid(x)

def _layernorm(x, axis=-1, eps=1e-05):
    m = jnp.mean(x, axis=axis, keepdims=True)
    v = jnp.var(x, axis=axis, keepdims=True)
    return (x - m) / jnp.sqrt(v + eps)

def _scatter_add(tgt, idx, src, axis=0):
    return tgt.at[idx].add(src)

def _segment_sum(src, seg, n):
    return jax.ops.segment_sum(src, seg, n)
kernel_name = 'mk_rec_standalone_d1_rec_r8_4cb43b'

def setup_inputs(seed: int=0):
    np.random.seed(seed)
    _w = jnp.asarray

    def _rec_inputs():
        import jax
        import jax.numpy as jnp
        _rk = jax.random.key(seed)
        r_inputs = -0.000207405 + 0.999984 * jax.random.normal(jax.random.fold_in(_rk, 1), (2048, 51, 128), jnp.float32)
        return r_inputs
    r_inputs = _rec_inputs()

    def _L0_rec_setup():
        import jax, jax.numpy as jnp
        import numpy as np
        B, T, D, U = (512, 50, 128, 128)
        ATT_H1, ATT_H2 = (128, 64)
        DH1, DH2 = (256, 128)
        BN_EPS = 0.001
        LEAKY = 0.0003

        def _gru(x_seq, W, Ur, b):
            Xp = jnp.einsum('btd,dk->btk', x_seq, W) + b[0]
            h0 = jnp.zeros((x_seq.shape[0], Ur.shape[0]), x_seq.dtype)

            def step(h, xp):
                hp = h @ Ur + b[1]
                xz, xr, xh = jnp.split(xp, 3, axis=-1)
                hz, hr, hh = jnp.split(hp, 3, axis=-1)
                z = jax.nn.sigmoid(xz + hz)
                r = jax.nn.sigmoid(xr + hr)
                hc = jnp.tanh(xh + r * hh)
                hn = z * h + (1.0 - z) * hc
                return (hn, hn)
            _, hs = jax.lax.scan(step, h0, jnp.swapaxes(Xp, 0, 1))
            return jnp.swapaxes(hs, 0, 1)
        key = jax.random.key(seed)
        ks = iter(jax.random.split(key, 40))
        n = lambda shape, s=0.05: jax.random.normal(next(ks), shape, dtype=jnp.float32) * s
        DI = U + D
        return {'inputs': n((B, T + 1, D), 1.0), 'gru_W': n((D, 3 * U)), 'gru_U': n((U, 3 * U)), 'gru_b': n((2, 3 * U)), 'att_W1': n((4 * U, ATT_H1)), 'att_b1': n((ATT_H1,)), 'att_W2': n((ATT_H1, ATT_H2)), 'att_b2': n((ATT_H2,)), 'att_W3': n((ATT_H2, 1)), 'att_b3': n((1,)), 'au_Wu': n((U, U)), 'au_bu': n((U,)), 'au_Uu': n((U, U)), 'au_Wr': n((U, U)), 'au_br': n((U,)), 'au_Ur': n((U, U)), 'au_Wc': n((U, U)), 'au_bc': n((U,)), 'au_Uc': n((U, U)), 'bn_gamma': jnp.ones((DI,), jnp.float32), 'bn_beta': jnp.zeros((DI,), jnp.float32), 'bn_mean': jnp.zeros((DI,), jnp.float32), 'bn_var': jnp.ones((DI,), jnp.float32), 'd_W1': n((DI, DH1)), 'd_b1': n((DH1,)), 'd_W2': n((DH1, DH2)), 'd_b2': n((DH2,)), 'f_W': n((DH2, 1)), 'f_b': n((1,))}
    _L0_rec_all = _L0_rec_setup()
    _L0_rec_in = {k: v for k, v in _L0_rec_all.items() if k in ('gru_W', 'gru_U', 'gru_b', 'att_W1', 'att_b1', 'att_W2', 'att_b2', 'att_W3', 'att_b3', 'au_Wu', 'au_bu', 'au_Uu', 'au_Wr', 'au_br', 'au_Ur', 'au_Wc', 'au_bc', 'au_Uc', 'bn_gamma', 'bn_beta', 'bn_mean', 'bn_var', 'd_W1', 'd_b1', 'd_W2', 'd_b2', 'f_W', 'f_b')}
    del _L0_rec_all
    return {'r_inputs': r_inputs, 'L0_rec_gru_W': _L0_rec_in['gru_W'], 'L0_rec_gru_U': _L0_rec_in['gru_U'], 'L0_rec_gru_b': _L0_rec_in['gru_b'], 'L0_rec_att_W1': _L0_rec_in['att_W1'], 'L0_rec_att_b1': _L0_rec_in['att_b1'], 'L0_rec_att_W2': _L0_rec_in['att_W2'], 'L0_rec_att_b2': _L0_rec_in['att_b2'], 'L0_rec_att_W3': _L0_rec_in['att_W3'], 'L0_rec_att_b3': _L0_rec_in['att_b3'], 'L0_rec_au_Wu': _L0_rec_in['au_Wu'], 'L0_rec_au_bu': _L0_rec_in['au_bu'], 'L0_rec_au_Uu': _L0_rec_in['au_Uu'], 'L0_rec_au_Wr': _L0_rec_in['au_Wr'], 'L0_rec_au_br': _L0_rec_in['au_br'], 'L0_rec_au_Ur': _L0_rec_in['au_Ur'], 'L0_rec_au_Wc': _L0_rec_in['au_Wc'], 'L0_rec_au_bc': _L0_rec_in['au_bc'], 'L0_rec_au_Uc': _L0_rec_in['au_Uc'], 'L0_rec_bn_gamma': _L0_rec_in['bn_gamma'], 'L0_rec_bn_beta': _L0_rec_in['bn_beta'], 'L0_rec_bn_mean': _L0_rec_in['bn_mean'], 'L0_rec_bn_var': _L0_rec_in['bn_var'], 'L0_rec_d_W1': _L0_rec_in['d_W1'], 'L0_rec_d_b1': _L0_rec_in['d_b1'], 'L0_rec_d_W2': _L0_rec_in['d_W2'], 'L0_rec_d_b2': _L0_rec_in['d_b2'], 'L0_rec_f_W': _L0_rec_in['f_W'], 'L0_rec_f_b': _L0_rec_in['f_b']}

def reference(r_inputs, L0_rec_gru_W, L0_rec_gru_U, L0_rec_gru_b, L0_rec_att_W1, L0_rec_att_b1, L0_rec_att_W2, L0_rec_att_b2, L0_rec_att_W3, L0_rec_att_b3, L0_rec_au_Wu, L0_rec_au_bu, L0_rec_au_Uu, L0_rec_au_Wr, L0_rec_au_br, L0_rec_au_Ur, L0_rec_au_Wc, L0_rec_au_bc, L0_rec_au_Uc, L0_rec_bn_gamma, L0_rec_bn_beta, L0_rec_bn_mean, L0_rec_bn_var, L0_rec_d_W1, L0_rec_d_b1, L0_rec_d_W2, L0_rec_d_b2, L0_rec_f_W, L0_rec_f_b):
    import jax
    import jax.numpy as jnp

    def _L0_rec_ref(inputs, gru_W, gru_U, gru_b, att_W1, att_b1, att_W2, att_b2, att_W3, att_b3, au_Wu, au_bu, au_Uu, au_Wr, au_br, au_Ur, au_Wc, au_bc, au_Uc, bn_gamma, bn_beta, bn_mean, bn_var, d_W1, d_b1, d_W2, d_b2, f_W, f_b):
        import jax, jax.numpy as jnp
        import numpy as np
        B, T, D, U = (512, 50, 128, 128)
        ATT_H1, ATT_H2 = (128, 64)
        DH1, DH2 = (256, 128)
        BN_EPS = 0.001
        LEAKY = 0.0003

        def _gru(x_seq, W, Ur, b):
            Xp = jnp.einsum('btd,dk->btk', x_seq, W) + b[0]
            h0 = jnp.zeros((x_seq.shape[0], Ur.shape[0]), x_seq.dtype)

            def step(h, xp):
                hp = h @ Ur + b[1]
                xz, xr, xh = jnp.split(xp, 3, axis=-1)
                hz, hr, hh = jnp.split(hp, 3, axis=-1)
                z = jax.nn.sigmoid(xz + hz)
                r = jax.nn.sigmoid(xr + hr)
                hc = jnp.tanh(xh + r * hh)
                hn = z * h + (1.0 - z) * hc
                return (hn, hn)
            _, hs = jax.lax.scan(step, h0, jnp.swapaxes(Xp, 0, 1))
            return jnp.swapaxes(hs, 0, 1)
        hist = inputs[:, :-1, :]
        news = inputs[:, -1, :]
        hs = _gru(hist, gru_W, gru_U, gru_b)
        news_b = jnp.broadcast_to(news[:, None, :], hs.shape)
        emb = jnp.concatenate([hs, news_b - hs, news_b, hs * news_b], axis=-1)
        a = jax.nn.relu(jnp.einsum('bti,ij->btj', emb, att_W1) + att_b1)
        a = jax.nn.relu(jnp.einsum('bti,ij->btj', a, att_W2) + att_b2)
        ats = jax.nn.sigmoid(jnp.einsum('bti,ij->btj', a, att_W3) + att_b3)
        xu = jnp.einsum('btd,dk->btk', hs, au_Wu) + au_bu
        xr = jnp.einsum('btd,dk->btk', hs, au_Wr) + au_br
        xc = jnp.einsum('btd,dk->btk', hs, au_Wc) + au_bc

        def au_step(h, xs):
            xu_t, xr_t, xc_t, at_t = xs
            u = jax.nn.sigmoid(xu_t + h @ au_Uu)
            r = jax.nn.sigmoid(xr_t + h @ au_Ur)
            c = jnp.tanh(xc_t + r * (h @ au_Uc))
            u_ = at_t * u
            hn = (1.0 - u_) * h + u_ * c
            return (hn, None)
        h0 = jnp.zeros_like(hs[:, 0, :])
        xs = (jnp.swapaxes(xu, 0, 1), jnp.swapaxes(xr, 0, 1), jnp.swapaxes(xc, 0, 1), jnp.swapaxes(ats, 0, 1))
        h_final, _ = jax.lax.scan(au_step, h0, xs)
        x = jnp.concatenate([h_final, news], axis=-1)
        x = (x - bn_mean) * jax.lax.rsqrt(bn_var + BN_EPS) * bn_gamma + bn_beta
        x = x @ d_W1 + d_b1
        x = jnp.where(x >= 0, x, LEAKY * x)
        x = x @ d_W2 + d_b2
        x = jnp.where(x >= 0, x, LEAKY * x)
        y = jax.nn.sigmoid(x @ f_W + f_b)
        return y
    y = _L0_rec_ref(r_inputs, L0_rec_gru_W, L0_rec_gru_U, L0_rec_gru_b, L0_rec_att_W1, L0_rec_att_b1, L0_rec_att_W2, L0_rec_att_b2, L0_rec_att_W3, L0_rec_att_b3, L0_rec_au_Wu, L0_rec_au_bu, L0_rec_au_Uu, L0_rec_au_Wr, L0_rec_au_br, L0_rec_au_Ur, L0_rec_au_Wc, L0_rec_au_bc, L0_rec_au_Uc, L0_rec_bn_gamma, L0_rec_bn_beta, L0_rec_bn_mean, L0_rec_bn_var, L0_rec_d_W1, L0_rec_d_b1, L0_rec_d_W2, L0_rec_d_b2, L0_rec_f_W, L0_rec_f_b)
    return y

_drawn_inputs = setup_inputs


def setup_inputs(seed=0):
    import zlib

    import numpy as np

    out = dict(_drawn_inputs(seed))
    spreads = {'L0_rec_bn_gamma': (1.0, 0.6),
     'L0_rec_bn_beta': (0.0, 0.8),
     'L0_rec_bn_mean': (0.0, 0.797),
     'L0_rec_bn_var': (1.0, 0.6)}
    factors = {'L0_rec_gru_W': 8.0,
     'L0_rec_gru_U': 8.0,
     'L0_rec_gru_b': 8.0,
     'L0_rec_att_W1': 8.0,
     'L0_rec_att_b1': 8.0,
     'L0_rec_att_W2': 8.0,
     'L0_rec_att_b2': 34.486,
     'L0_rec_att_W3': 8.0,
     'L0_rec_au_Wu': 8.0,
     'L0_rec_au_bu': 22.207,
     'L0_rec_au_Uu': 8.0,
     'L0_rec_au_Wr': 8.0,
     'L0_rec_au_br': 31.238,
     'L0_rec_au_Ur': 8.0,
     'L0_rec_au_Wc': 8.0,
     'L0_rec_au_bc': 8.0,
     'L0_rec_au_Uc': 8.0,
     'L0_rec_d_b1': 7.849,
     'L0_rec_d_b2': 8.0}
    for name, (base, spread) in spreads.items():
        noise = np.random.default_rng([zlib.crc32(name.encode()), seed]).standard_normal(out[name].shape)
        drawn = base * np.exp(spread * noise) if base else spread * noise
        out[name] = jnp.asarray(drawn.astype(out[name].dtype))
    for name, factor in factors.items():
        out[name] = (out[name] * factor).astype(out[name].dtype)
    return out
```

```python
from contextlib import ExitStack

import concourse.bass as bass
from concourse import mybir

ALU = mybir.AluOpType
ACT = mybir.ActivationFunctionType
F32 = mybir.dt.float32
F16 = mybir.dt.float16

P = 128
CH = 512
NC = 4
LEAKY = 0.0003
BN_EPS = 0.001

B_R, B_HH, B_Z, B_XH, B_A, B_AR, B_AHC, B_AXC = range(8)
B_A1 = B_A2 = B_A
B_LG = B_XH
B_AU = B_Z

W_Z, W_R, W_H, U_Z, U_R, U_H, A_HS, AW_U, AW_R, AW_C, AU_U, AU_R, AU_C = range(13)
NW = 13


def rec_kernel(nc, xs, gru_W, gru_U, gru_b, att_W1, att_b1, att_W2, att_b2, att_W3, att_b3,
               au_Wu, au_bu, au_Uu, au_Wr, au_br, au_Ur, au_Wc, au_bc, au_Uc,
               bn, d_W1, d_b1, d_W2, d_b2, f_W, f_b, out):
    T = xs.shape[0] - 1
    NB = xs.shape[2]
    assert NB == NC * CH and xs.shape[1] == P
    ITEMS = NC * T
    FIRST = -2
    LOOP_LO = 2 * NC
    LOOP_HI = ITEMS - NC
    LAST = ITEMS + NC

    with ExitStack() as ctx:
        def sb(name, shape, dt=F32):
            return ctx.enter_context(nc.sbuf_tensor(name, shape, dt))

        def sem(name):
            return ctx.enter_context(nc.semaphore(name))

        w32 = sb("w32", [P, NW, P])
        w_hi = sb("w_hi", [P, NW, P], F16)
        w_lo = sb("w_lo", [P, NW, P], F16)
        w1 = sb("w1", [P, 4, P])
        w1_news = sb("w1_news", [P, P])
        w2 = sb("w2", [P, 2, 64])
        w3 = sb("w3", [P, 1])
        w3_rep = sb("w3_rep", [P, P])
        ones = sb("ones", [P, P])
        dw1 = sb("dw1", [P, 2, 2 * P])
        dw2 = sb("dw2", [P, 2, P])
        fw = sb("fw", [P, 1])
        gb = sb("gb", [P, 6])
        b_zr = sb("b_zr", [P, 2])
        b_att1 = sb("b_att1", [P, 1])
        b_att2 = sb("b_att2", [P, 1])
        b_att3 = sb("b_att3", [P, 1])
        b_au = sb("b_au", [P, 3])
        b_d1 = sb("b_d1", [P, 2])
        b_d2 = sb("b_d2", [P, 1])
        b_f = sb("b_f", [1, 1])
        bn_in = sb("bn_in", [P, 8])
        bn_t = sb("bn_t", [P, 6, 2])
        x32 = sb("x32", [P, NC, CH])
        x_hi = sb("x_hi", [P, NC, CH], F16)
        x_lo = sb("x_lo", [P, NC, CH], F16)
        h32 = sb("h32", [P, NC, CH])
        h_hi = sb("h_hi", [P, NC, CH], F16)
        h_lo = sb("h_lo", [P, NC, CH], F16)
        g32 = sb("g32", [P, NC, CH])
        g_hi = sb("g_hi", [P, NC, CH], F16)
        g_lo = sb("g_lo", [P, NC, CH], F16)
        news = sb("news", [P, NC, CH])
        news_bn = sb("news_bn", [P, NC, CH])
        c_news = sb("c_news", [P, NC, CH])
        score = sb("score", [P, NC, CH])
        r = sb("r", [P, 2, CH])
        z = sb("z", [P, 2, CH])
        t = sb("t", [P, 2, CH])
        hc = sb("hc", [P, 2, CH])
        d = sb("d", [P, CH])
        hn = sb("hn", [P, 2, CH])
        a1p = sb("a1p", [P, 2, CH])
        a1 = sb("a1", [P, 2, CH])
        a2 = sb("a2", [P, 2, CH])
        gr = sb("gr", [P, 2, CH])
        gu = sb("gu", [P, 2, CH])
        gt = sb("gt", [P, 2, CH])
        gc = sb("gc", [P, 2, CH])
        gus = sb("gus", [P, 2, CH])
        gd = sb("gd", [P, CH])
        g_bn = sb("g_bn", [P, NC, CH])
        y1p = sb("y1p", [P, 2, 2, CH])
        y1 = sb("y1", [P, 2, 2, CH])
        y2p = sb("y2p", [P, 2, CH])
        y2 = sb("y2", [P, 2, CH])
        y = sb("y", [1, NB])
        ps = ctx.enter_context(nc.psum_tensor("ps", [P, 8, CH], F32))

        w_landed = sem("w_landed")
        news_landed = sem("news_landed")
        x_landed = [sem(f"x_landed{c}") for c in range(NC)]
        zeroed = sem("zeroed")
        w_prep = sem("w_prep")
        w_ready = sem("w_ready")
        sqrt_done = sem("sqrt_done")
        bn_ready = sem("bn_ready")
        news_pe = sem("news_pe")
        c_ready = sem("c_ready")
        x_split = sem("x_split")
        xhi_ready = sem("xhi_ready")
        r_pe, hh_pe, z_pe, xh_pe = sem("r_pe"), sem("hh_pe"), sem("z_pe"), sem("xh_pe")
        r_ready, z_ready, hc_ready = sem("r_ready"), sem("z_ready"), sem("hc_ready")
        t1_ready, t2_ready = sem("t1_ready"), sem("t2_ready")
        d_ready, e_ready, h_ready = sem("d_ready"), sem("e_ready"), sem("h_ready")
        hhi_ready, hlo_ready = sem("hhi_ready"), sem("hlo_ready")
        hn_ready = sem("hn_ready")
        a1_pe, a1p_ready, a1_ready = sem("a1_pe"), sem("a1p_ready"), sem("a1_ready")
        a2_pe, a2_ready = sem("a2_pe"), sem("a2_ready")
        lg_pe, score_ready = sem("lg_pe"), sem("score_ready")
        gr_pe, ghc_pe, gxc_pe, gu_pe = sem("gr_pe"), sem("ghc_pe"), sem("gxc_pe"), sem("gu_pe")
        gr_ready, gu_ready, gc_ready = sem("gr_ready"), sem("gu_ready"), sem("gc_ready")
        gt1_ready, gt2_ready, gus_ready = sem("gt1_ready"), sem("gt2_ready"), sem("gus_ready")
        gd_ready, ge_ready, g_ready = sem("gd_ready"), sem("ge_ready"), sem("g_ready")
        ghi_ready, glo_ready = sem("ghi_ready"), sem("glo_ready")
        gbn_ready = sem("gbn_ready")
        d1_pe, y1p_ready, y1_ready = sem("d1_pe"), sem("y1p_ready"), sem("y1_ready")
        d2_pe, y2p_ready, y2_ready = sem("d2_pe"), sem("y2p_ready"), sem("y2_ready")
        f_pe, y_ready, y_stored = sem("f_pe"), sem("y_ready"), sem("y_stored")

        w_loads = [
            (w32[:, W_Z:W_H + 1, :], gru_W.rearrange("p (k m) -> p k m", k=3)),
            (w32[:, U_Z:U_H + 1, :], gru_U.rearrange("p (k m) -> p k m", k=3)),
            (w32[:, AW_U, :], au_Wu), (w32[:, AW_R, :], au_Wr), (w32[:, AW_C, :], au_Wc),
            (w32[:, AU_U, :], au_Uu), (w32[:, AU_R, :], au_Ur), (w32[:, AU_C, :], au_Uc),
            (w1[:, :, :], att_W1.rearrange("(k p) m -> p k m", p=P)),
            (w2[:, 0, :], att_W2), (w2[:, 1, :], att_W2),
            (w3[0:64, :], att_W3), (w3[64:128, :], att_W3),
            (b_att2[0:64, :], att_b2), (b_att2[64:128, :], att_b2),
            (gb[:, :], gru_b), (b_att1[:, :], att_b1), (b_att3[:, :], att_b3),
            (b_au[:, 0:1], au_bu), (b_au[:, 1:2], au_br), (b_au[:, 2:3], au_bc),
            (bn_in[:, :], bn),
            (dw1[:, :, :], d_W1.rearrange("(k p) m -> p k m", p=P)),
            (dw2[:, :, :], d_W2.rearrange("(k p) m -> p k m", p=P)),
            (fw[:, :], f_W), (b_d1[:, :], d_b1), (b_d2[:, :], d_b2), (b_f[:, :], f_b),
        ]
        W_LANDED = 16 * len(w_loads)

        def has(item):
            return 0 <= item < ITEMS

        block = ctx.enter_context(nc.Block())

        @block.sync
        def _(sp):
            for c in range(2):
                sp.dma_start(x32[:, c, :], xs[0, :, c * CH:(c + 1) * CH]).then_inc(x_landed[c], 16)
            for dst, src in w_loads[:len(w_loads) // 2]:
                sp.dma_start(dst, src).then_inc(w_landed, 16)
            sp.dma_start(news[:, :, :], xs[T, :, :].rearrange("p (c n) -> p c n", c=NC)).then_inc(news_landed, 16)
            for c in range(2, NC):
                sp.dma_start(x32[:, c, :], xs[0, :, c * CH:(c + 1) * CH]).then_inc(x_landed[c], 16)
            with sp.Fori(1, T) as step:
                for c in range(NC):
                    sp.wait_ge(x_split, 4 * step + c - 3)
                    sp.dma_start(x32[:, c, :], xs[step, :, c * CH:(c + 1) * CH]).then_inc(x_landed[c], 16)
            sp.wait_ge(y_ready, NC)
            sp.dma_start(out, y[:, :]).then_inc(y_stored, 16)
            sp.wait_ge(y_stored, 16)

        @block.gpsimd
        def _(pool):
            g = nc.gpsimd
            for state in (h32, h_hi, h_lo, g32, g_hi, g_lo):
                g.memset(state[:, :, :], 0.0).then_inc(zeroed, 1)
            g.memset(ones[:, :], 1.0).then_inc(zeroed, 1)

            def slot(s, low):
                c = low % NC
                if has(low + 2):
                    c2 = (low + 2) % NC
                    pool.wait_ge(xhi_ready, s + 3)
                    g.tensor_tensor(x_lo[:, c2, :], x32[:, c2, :], x_hi[:, c2, :], ALU.subtract).then_inc(x_split, 1)
                if has(low):
                    if low == 0:
                        pool.wait_ge(news_landed, 16)
                    pool.wait_ge(h_ready, s + 1)
                    g.tensor_tensor(hn[:, low % 2, :], h32[:, c, :], news[:, c, :], ALU.mult).then_inc(hn_ready, 1)
                if has(low - 4):
                    pool.wait_ge(score_ready, s - 3)
                    pool.wait_ge(gu_ready, s - 3)
                    g.tensor_tensor(gus[:, low % 2, :], gu[:, low % 2, :], score[:, c, :], ALU.mult).then_inc(gus_ready, 1)

            for s in range(FIRST, LOOP_LO):
                slot(s, s)
            with pool.Fori(LOOP_LO, LOOP_HI, NC) as s0:
                for c in range(NC):
                    slot(s0 + c, LOOP_LO + c)
            for s in range(LOOP_HI, LAST):
                slot(s, s)

        @block.scalar
        def _(act):
            a = nc.scalar
            for dst, src in w_loads[len(w_loads) // 2:]:
                act.dma_start(dst, src).then_inc(w_landed, 16)
            act.wait_ge(w_prep, 4)
            a.activation(bn_t[:, 1, :], bn_t[:, 0, :], ACT.Sqrt).then_inc(sqrt_done, 1)
            act.wait_ge(w_ready, 1)

            def slot(s, low):
                c = low % NC
                if has(low + 2):
                    c2 = (low + 2) % NC
                    act.wait_ge(x_landed[c2], 4 * (s + 2 - c2) + 16)
                    if low - 2 >= 0:
                        act.wait_ge(xh_pe, s - 1)
                    a.activation(x_hi[:, c2, :], x32[:, c2, :], ACT.Copy).then_inc(xhi_ready, 1)
                if has(low - 2):
                    act.wait_ge(a1p_ready, s - 1)
                    a.activation(a1[:, low % 2, :], a1p[:, low % 2, :], ACT.Relu).then_inc(a1_ready, 1)
                if has(low - 3):
                    act.wait_ge(lg_pe, s - 2)
                    a.activation(score[:, (low - 3) % NC, :], ps[:, B_LG, :], ACT.Sigmoid,
                                 bias=b_att3[:, :]).then_inc(score_ready, 1)
                if has(low):
                    act.wait_ge(r_pe, s + 1)
                    a.activation(r[:, low % 2, :], ps[:, B_R, :], ACT.Sigmoid, bias=b_zr[:, 1:2]).then_inc(r_ready, 1)
                if has(low - 5):
                    act.wait_ge(g_ready, s - 4)
                    a.activation(g_hi[:, (low - 5) % NC, :], g32[:, (low - 5) % NC, :], ACT.Copy).then_inc(ghi_ready, 1)
                if has(low):
                    act.wait_ge(z_pe, s + 1)
                    a.activation(z[:, low % 2, :], ps[:, B_Z, :], ACT.Sigmoid, bias=b_zr[:, 0:1]).then_inc(z_ready, 1)
                    act.wait_ge(t2_ready, s + 1)
                    a.activation(hc[:, low % 2, :], t[:, low % 2, :], ACT.Tanh, bias=gb[:, 2:3]).then_inc(hc_ready, 1)
                if has(low - 2):
                    act.wait_ge(a2_pe, s - 1)
                    a.activation(a2[:, low % 2, :], ps[:, B_A2, :], ACT.Relu, bias=b_att2[:, :]).then_inc(a2_ready, 1)
                if has(low - 4):
                    act.wait_ge(gr_pe, s - 3)
                    a.activation(gr[:, low % 2, :], ps[:, B_AR, :], ACT.Sigmoid, bias=b_au[:, 1:2]).then_inc(gr_ready, 1)
                    act.wait_ge(gu_pe, s - 3)
                    a.activation(gu[:, low % 2, :], ps[:, B_AU, :], ACT.Sigmoid, bias=b_au[:, 0:1]).then_inc(gu_ready, 1)
                    act.wait_ge(gt2_ready, s - 3)
                    a.activation(gc[:, low % 2, :], gt[:, low % 2, :], ACT.Tanh, bias=b_au[:, 2:3]).then_inc(gc_ready, 1)
                if has(low):
                    act.wait_ge(h_ready, s + 1)
                    a.activation(h_hi[:, c, :], h32[:, c, :], ACT.Copy).then_inc(hhi_ready, 1)

            for s in range(FIRST, LOOP_LO):
                slot(s, s)
            with act.Fori(LOOP_LO, LOOP_HI, NC) as s0:
                for c in range(NC):
                    slot(s0 + c, LOOP_LO + c)
            for s in range(LOOP_HI, LAST):
                slot(s, s)
            for c in range(NC):
                for m in range(2):
                    act.wait_ge(d1_pe, 2 * c + m + 1)
                    a.activation(y1p[:, c % 2, m, :], ps[:, 4 * (c % 2) + m, :], ACT.Identity,
                                 bias=b_d1[:, m:m + 1]).then_inc(y1p_ready, 1)
                act.wait_ge(d2_pe, c + 1)
                a.activation(y2p[:, c % 2, :], ps[:, 4 * (c % 2) + 2, :], ACT.Identity,
                             bias=b_d2[:, :]).then_inc(y2p_ready, 1)
                act.wait_ge(f_pe, c + 1)
                a.activation(y[0:1, c * CH:(c + 1) * CH], ps[0:1, 4 * (c % 2) + 3, :], ACT.Sigmoid,
                             bias=b_f[:, :]).then_inc(y_ready, 1)

        @block.vector
        def _(dve):
            v = nc.vector
            dve.wait_ge(w_landed, W_LANDED)
            dve.wait_ge(zeroed, 7)
            v.tensor_tensor(w32[:, A_HS, :], w1[:, 0, :], w1[:, 1, :], ALU.subtract).then_inc(w_prep, 1)
            v.tensor_tensor(w1_news[:, :], w1[:, 1, :], w1[:, 2, :], ALU.add).then_inc(w_prep, 1)
            v.tensor_tensor(b_zr[:, :], gb[:, 0:2], gb[:, 3:5], ALU.add).then_inc(w_prep, 1)
            v.tensor_scalar(bn_t[:, 0, :], bn_in[:, 6:8], BN_EPS, None, ALU.add).then_inc(w_prep, 1)
            v.tensor_scalar(w3_rep[:, :], ones[:, :], w3[:, 0:1], 0.5, ALU.mult, ALU.mult).then_inc(w_prep, 1)
            dve.wait_ge(w_prep, 5)
            v.tensor_copy(w_hi[:, :, :], w32[:, :, :]).then_inc(w_prep, 1)
            dve.wait_ge(w_prep, 6)
            v.tensor_tensor(w_lo[:, :, :], w32[:, :, :], w_hi[:, :, :], ALU.subtract).then_inc(w_ready, 1)
            for c in range(NC):
                dve.wait_ge(news_pe, c + 1)
                v.tensor_scalar(c_news[:, c, :], ps[:, B_AR + c % 2, :], b_att1[:, 0:1], None, ALU.add).then_inc(c_ready, 1)
            dve.wait_ge(sqrt_done, 1)
            v.reciprocal(bn_t[:, 2, :], bn_t[:, 1, :]).then_inc(bn_ready, 1)
            dve.wait_ge(bn_ready, 1)
            v.tensor_tensor(bn_t[:, 3, :], bn_t[:, 2, :], bn_t[:, 2, :], ALU.mult).then_inc(bn_ready, 1)
            dve.wait_ge(bn_ready, 2)
            v.tensor_tensor(bn_t[:, 3, :], bn_t[:, 3, :], bn_t[:, 0, :], ALU.mult).then_inc(bn_ready, 1)
            dve.wait_ge(bn_ready, 3)
            v.tensor_scalar(bn_t[:, 3, :], bn_t[:, 3, :], -0.5, 1.5, ALU.mult, ALU.add).then_inc(bn_ready, 1)
            dve.wait_ge(bn_ready, 4)
            v.tensor_tensor(bn_t[:, 3, :], bn_t[:, 3, :], bn_t[:, 2, :], ALU.mult).then_inc(bn_ready, 1)
            dve.wait_ge(bn_ready, 5)
            v.tensor_tensor(bn_t[:, 4, :], bn_t[:, 3, :], bn_in[:, 0:2], ALU.mult).then_inc(bn_ready, 1)
            dve.wait_ge(bn_ready, 6)
            v.tensor_tensor(bn_t[:, 3, :], bn_in[:, 4:6], bn_t[:, 4, :], ALU.mult).then_inc(bn_ready, 1)
            dve.wait_ge(bn_ready, 7)
            v.tensor_tensor(bn_t[:, 5, :], bn_in[:, 2:4], bn_t[:, 3, :], ALU.subtract).then_inc(bn_ready, 1)
            dve.wait_ge(bn_ready, 8)
            v.tensor_scalar(news_bn[:, :, :], news[:, :, :], bn_t[:, 4, 1:2], bn_t[:, 5, 1:2],
                            ALU.mult, ALU.add).then_inc(bn_ready, 1)

            def slot(s, low):
                c = low % NC
                if has(low - 5):
                    q, k = (low - 5) % NC, (low - 5) % 2
                    dve.wait_ge(gc_ready, s - 4)
                    v.tensor_tensor(gd[:, :], gc[:, k, :], g32[:, q, :], ALU.subtract).then_inc(gd_ready, 1)
                    dve.wait_ge(gus_ready, s - 4)
                    dve.wait_ge(gd_ready, s - 4)
                    v.tensor_tensor(gd[:, :], gd[:, :], gus[:, k, :], ALU.mult).then_inc(ge_ready, 1)
                    dve.wait_ge(ge_ready, s - 4)
                    v.tensor_tensor(g32[:, q, :], g32[:, q, :], gd[:, :], ALU.add).then_inc(g_ready, 1)
                if has(low):
                    dve.wait_ge(hh_pe, s + 1)
                    dve.wait_ge(r_ready, s + 1)
                    v.scalar_tensor_tensor(out=t[:, low % 2, :], in0=ps[:, B_HH, :], scalar=gb[:, 5:6],
                                           in1=r[:, low % 2, :], op0=ALU.add, op1=ALU.mult).then_inc(t1_ready, 1)
                if has(low - 5):
                    dve.wait_ge(ghi_ready, s - 4)
                    v.tensor_tensor(g_lo[:, q, :], g32[:, q, :], g_hi[:, q, :], ALU.subtract).then_inc(glo_ready, 1)
                if has(low):
                    dve.wait_ge(xh_pe, s + 1)
                    dve.wait_ge(t1_ready, s + 1)
                    v.tensor_tensor(t[:, low % 2, :], t[:, low % 2, :], ps[:, B_XH, :], ALU.add).then_inc(t2_ready, 1)
                    dve.wait_ge(hc_ready, s + 1)
                    v.tensor_tensor(d[:, :], h32[:, c, :], hc[:, low % 2, :], ALU.subtract).then_inc(d_ready, 1)
                    dve.wait_ge(z_ready, s + 1)
                    dve.wait_ge(d_ready, s + 1)
                    v.tensor_tensor(d[:, :], d[:, :], z[:, low % 2, :], ALU.mult).then_inc(e_ready, 1)
                    dve.wait_ge(e_ready, s + 1)
                    v.tensor_tensor(h32[:, c, :], hc[:, low % 2, :], d[:, :], ALU.add).then_inc(h_ready, 1)
                if has(low - 4):
                    dve.wait_ge(ghc_pe, s - 3)
                    dve.wait_ge(gr_ready, s - 3)
                    v.tensor_tensor(gt[:, low % 2, :], gr[:, low % 2, :], ps[:, B_AHC, :], ALU.mult).then_inc(gt1_ready, 1)
                    dve.wait_ge(gxc_pe, s - 3)
                    dve.wait_ge(gt1_ready, s - 3)
                    v.tensor_tensor(gt[:, low % 2, :], gt[:, low % 2, :], ps[:, B_AXC, :], ALU.add).then_inc(gt2_ready, 1)
                if has(low - 1):
                    dve.wait_ge(a1_pe, s)
                    v.tensor_tensor(a1p[:, (low - 1) % 2, :], c_news[:, (low - 1) % NC, :], ps[:, B_A1, :],
                                    ALU.add).then_inc(a1p_ready, 1)
                if has(low):
                    dve.wait_ge(hhi_ready, s + 1)
                    v.tensor_tensor(h_lo[:, c, :], h32[:, c, :], h_hi[:, c, :], ALU.subtract).then_inc(hlo_ready, 1)

            for s in range(0, LOOP_LO):
                slot(s, s)
            with dve.Fori(LOOP_LO, LOOP_HI, NC) as s0:
                for c in range(NC):
                    slot(s0 + c, LOOP_LO + c)
            for s in range(LOOP_HI, LAST):
                slot(s, s)
            c, k = (ITEMS - 1) % NC, (ITEMS - 1) % 2
            dve.wait_ge(gc_ready, ITEMS)
            v.tensor_tensor(gd[:, :], gc[:, k, :], g32[:, c, :], ALU.subtract).then_inc(gd_ready, 1)
            dve.wait_ge(gus_ready, ITEMS)
            dve.wait_ge(gd_ready, ITEMS)
            v.tensor_tensor(gd[:, :], gd[:, :], gus[:, k, :], ALU.mult).then_inc(ge_ready, 1)
            dve.wait_ge(ge_ready, ITEMS)
            v.tensor_tensor(g32[:, c, :], g32[:, c, :], gd[:, :], ALU.add).then_inc(g_ready, 1)
            for c in range(NC):
                dve.wait_ge(bn_ready, 9)
                dve.wait_ge(g_ready, ITEMS - NC + c + 1)
                v.tensor_scalar(g_bn[:, c, :], g32[:, c, :], bn_t[:, 4, 0:1], bn_t[:, 5, 0:1],
                                ALU.mult, ALU.add).then_inc(gbn_ready, 1)
            for c in range(NC):
                for m in range(2):
                    dve.wait_ge(y1p_ready, 2 * c + m + 1)
                    v.scalar_tensor_tensor(out=y1[:, c % 2, m, :], in0=y1p[:, c % 2, m, :], scalar=LEAKY,
                                           in1=y1p[:, c % 2, m, :], op0=ALU.mult, op1=ALU.max).then_inc(y1_ready, 1)
                dve.wait_ge(y2p_ready, c + 1)
                v.scalar_tensor_tensor(out=y2[:, c % 2, :], in0=y2p[:, c % 2, :], scalar=LEAKY,
                                       in1=y2p[:, c % 2, :], op0=ALU.mult, op1=ALU.max).then_inc(y2_ready, 1)

        @block.tensor
        def _(pe):
            m = nc.tensor

            def split_product(bank, w, hi, lo, start, stop):
                m.matmul(ps[:, bank, :], w_hi[:, w, :], hi, start=start, stop=False)
                m.matmul(ps[:, bank, :], w_hi[:, w, :], lo, start=False, stop=False)
                return m.matmul(ps[:, bank, :], w_lo[:, w, :], hi, start=False, stop=stop)

            pe.wait_ge(w_ready, 1)
            pe.wait_ge(news_landed, 16)
            for c in range(NC):
                if c >= 2:
                    pe.wait_ge(c_ready, c - 1)
                m.matmul(ps[:, B_AR + c % 2, :], w1_news[:, :], news[:, c, :], start=True, stop=True).then_inc(news_pe, 1)

            def slot(s, low):
                c = low % NC
                p = (low - 1) % NC
                if has(low):
                    x = (x_hi[:, c, :], x_lo[:, c, :])
                    h = (h_hi[:, c, :], h_lo[:, c, :])
                    pe.wait_ge(x_split, s + 1)
                    if low >= 1:
                        pe.wait_ge(r_ready, s)
                    split_product(B_R, W_R, *x, start=True, stop=False)
                    if low >= 4:
                        pe.wait_ge(hlo_ready, s - 3)
                    split_product(B_R, U_R, *h, start=False, stop=True).then_inc(r_pe, 1)
                    if low >= 1:
                        pe.wait_ge(t1_ready, s)
                    split_product(B_HH, U_H, *h, start=True, stop=True).then_inc(hh_pe, 1)
                    if low >= 5:
                        pe.wait_ge(gu_ready, s - 4)
                    elif low >= 1:
                        pe.wait_ge(z_ready, s)
                    split_product(B_Z, W_Z, *x, start=True, stop=False)
                    split_product(B_Z, U_Z, *h, start=False, stop=True).then_inc(z_pe, 1)
                    if low >= 3:
                        pe.wait_ge(score_ready, s - 2)
                    elif low >= 1:
                        pe.wait_ge(t2_ready, s)
                    split_product(B_XH, W_H, *x, start=True, stop=True).then_inc(xh_pe, 1)
                if has(low - 2):
                    pe.wait_ge(a1_ready, s - 1)
                    m.matmul(ps[:, B_A2, :], w2[:, :, :].rearrange("p a b -> p (a b)"), a1[:, low % 2, :],
                             start=True, stop=True).then_inc(a2_pe, 1)
                if has(low - 4):
                    h = (h_hi[:, c, :], h_lo[:, c, :])
                    g = (g_hi[:, c, :], g_lo[:, c, :])
                    if low >= 5:
                        pe.wait_ge(gr_ready, s - 4)
                    split_product(B_AR, AW_R, *h, start=True, stop=False)
                    if low >= 8:
                        pe.wait_ge(glo_ready, s - 7)
                    split_product(B_AR, AU_R, *g, start=False, stop=True).then_inc(gr_pe, 1)
                    if low >= 5:
                        pe.wait_ge(gt1_ready, s - 4)
                    split_product(B_AHC, AU_C, *g, start=True, stop=True).then_inc(ghc_pe, 1)
                    if low >= 5:
                        pe.wait_ge(gt2_ready, s - 4)
                    split_product(B_AXC, AW_C, *h, start=True, stop=True).then_inc(gxc_pe, 1)
                    if has(low):
                        pe.wait_ge(z_ready, s + 1)
                    else:
                        pe.wait_ge(gu_ready, s - 4)
                    split_product(B_AU, AW_U, *h, start=True, stop=False)
                    split_product(B_AU, AU_U, *g, start=False, stop=True).then_inc(gu_pe, 1)
                if has(low - 1):
                    if low >= 2:
                        pe.wait_ge(a2_ready, s - 1)
                    pe.wait_ge(hlo_ready, s)
                    split_product(B_A1, A_HS, h_hi[:, p, :], h_lo[:, p, :], start=True, stop=False)
                    pe.wait_ge(hn_ready, s)
                    m.matmul(ps[:, B_A1, :], w1[:, 3, :], hn[:, (low - 1) % 2, :],
                             start=False, stop=True).then_inc(a1_pe, 1)
                if has(low - 2):
                    pe.wait_ge(a2_ready, s - 1)
                    if has(low):
                        pe.wait_ge(t2_ready, s + 1)
                    else:
                        pe.wait_ge(score_ready, s - 2)
                    m.matmul(ps[:, B_LG, :], w3_rep[:, :], a2[:, low % 2, :], start=True, stop=True).then_inc(lg_pe, 1)

            for s in range(0, LOOP_LO):
                slot(s, s)
            with pe.Fori(LOOP_LO, LOOP_HI, NC) as s0:
                for c in range(NC):
                    slot(s0 + c, LOOP_LO + c)
            for s in range(LOOP_HI, LAST):
                slot(s, s)

            for c in range(NC):
                b = 4 * (c % 2)
                pe.wait_ge(gbn_ready, NC if c == 0 else c + 1)
                for k in range(2):
                    if c >= 2:
                        pe.wait_ge(y1p_ready, 2 * (c - 2) + k + 1)
                    m.matmul(ps[:, b + k, :], dw1[:, 0, k * P:(k + 1) * P], g_bn[:, c, :], start=True, stop=False)
                    m.matmul(ps[:, b + k, :], dw1[:, 1, k * P:(k + 1) * P], news_bn[:, c, :],
                             start=False, stop=True).then_inc(d1_pe, 1)
                pe.wait_ge(y1_ready, 2 * c + 2)
                m.matmul(ps[:, b + 2, :], dw2[:, 0, :], y1[:, c % 2, 0, :], start=True, stop=False)
                m.matmul(ps[:, b + 2, :], dw2[:, 1, :], y1[:, c % 2, 1, :], start=False, stop=True).then_inc(d2_pe, 1)
                pe.wait_ge(y2_ready, c + 1)
                m.matmul(ps[0:1, b + 3, :], fw[:, :], y2[:, c % 2, :], start=True, stop=True).then_inc(f_pe, 1)


def kernel(**inputs):
    import numpy as np
    import concourse.bacc as bacc
    from concourse.bass_utils import run_bass_kernel_spmd

    w = {k[len("L0_rec_"):]: np.asarray(v) for k, v in inputs.items() if k != "r_inputs"}
    x = np.asarray(inputs["r_inputs"])

    def columns(v):
        return np.ascontiguousarray(v.reshape(-1, P).T)

    bn = np.concatenate([columns(w[k]) for k in ("bn_gamma", "bn_beta", "bn_mean", "bn_var")], axis=1)
    arrays = {
        "xs": np.ascontiguousarray(x.transpose(1, 2, 0)),
        "gru_W": w["gru_W"], "gru_U": w["gru_U"], "gru_b": columns(w["gru_b"]),
        "att_W1": w["att_W1"], "att_b1": w["att_b1"].reshape(P, 1), "att_W2": w["att_W2"],
        "att_b2": w["att_b2"].reshape(64, 1), "att_W3": w["att_W3"],
        "att_b3": np.ascontiguousarray(np.broadcast_to(w["att_b3"].reshape(1, 1), (P, 1))),
        "au_Wu": w["au_Wu"], "au_bu": w["au_bu"].reshape(P, 1), "au_Uu": w["au_Uu"],
        "au_Wr": w["au_Wr"], "au_br": w["au_br"].reshape(P, 1), "au_Ur": w["au_Ur"],
        "au_Wc": w["au_Wc"], "au_bc": w["au_bc"].reshape(P, 1), "au_Uc": w["au_Uc"],
        "bn": bn, "d_W1": w["d_W1"], "d_b1": columns(w["d_b1"]), "d_W2": w["d_W2"],
        "d_b2": w["d_b2"].reshape(P, 1), "f_W": w["f_W"], "f_b": w["f_b"].reshape(1, 1),
    }
    nc = bacc.Bacc("TRN2", target_bir_lowering=False, num_devices=1)
    feed, args = {}, []
    for name, value in arrays.items():
        value = np.ascontiguousarray(value)
        feed[f"in_{name}"] = value
        args.append(nc.dram_tensor(f"in_{name}", value.shape, mybir.dt.from_np(value.dtype), kind="ExternalInput").ap())
    out = nc.dram_tensor("out_y", (1, x.shape[0]), F32, kind="ExternalOutput").ap()
    rec_kernel(nc, *args, out)
    result = run_bass_kernel_spmd(nc, [feed], core_ids=[0])
    return result.results[0]["out_y"].reshape(x.shape[0], 1)
```

```python
from contextlib import ExitStack

import concourse.bass as bass
from concourse import mybir

ALU = mybir.AluOpType
ACT = mybir.ActivationFunctionType
F32 = mybir.dt.float32
F16 = mybir.dt.float16

P = 128
H = P // 2
CH = 512
NC = 4
LEAKY = 0.0003
BN_EPS = 0.001

B_GHH, B_A1, B_Z, B_R, B_A2, B_HH, B_GR, B_GXH = range(8)
B_XH = B_R
B_SCORE = B_Z
B_GU = B_A2
B_NEWS = (B_GR, B_GHH)
B_D1, B_D2, B_F = (B_HH, B_R), B_Z, B_A1

W_R, W_Z, W_H, U_R, U_Z, U_H, A_HS, A_HN, A_2, GW_R, GW_U, GW_C, GU_R, GU_U, GU_C = range(15)
NW = 15


def rec_kernel(nc, xs, gru_W, gru_U, gru_b, att_W1, att_b1, att_W2, att_b2, att_W3, att_b3,
               au_Wu, au_bu, au_Uu, au_Wr, au_br, au_Ur, au_Wc, au_bc, au_Uc,
               bn, d_W1, d_b1, d_W2, d_b2, f_W, f_b, out):
    T = xs.shape[0] - 1
    NB = xs.shape[2]
    assert NB == NC * CH and xs.shape[1] == P
    ITEMS = NC * T
    FIRST = -3
    LOOP_LO = 3 * NC
    LOOP_HI = ITEMS - NC
    HEAD = ITEMS + 2
    LAST = HEAD + NC + 2

    def has(item):
        return 0 <= item < ITEMS

    with ExitStack() as ctx:
        def sb(name, shape, dt=F32):
            return ctx.enter_context(nc.sbuf_tensor(name, shape, dt))

        def sem(name):
            return ctx.enter_context(nc.semaphore(name))

        w32 = sb("w32", [P, NW, P])
        w_hi = sb("w_hi", [P, NW, P], F16)
        w_lo = sb("w_lo", [P, NW, P], F16)
        w1 = sb("w1", [P, 3, P])
        w1_news = sb("w1_news", [P, P])
        w2_sum = sb("w2_sum", [P, 2, P], F16)
        w3 = sb("w3", [P, 1])
        w3_rep = sb("w3_rep", [P, P])
        w3_hi = sb("w3_hi", [P, P], F16)
        w3_lo = sb("w3_lo", [P, P], F16)
        ones = sb("ones", [P, P])
        dw1 = sb("dw1", [P, 2, 2 * P])
        dw2 = sb("dw2", [P, 2, P])
        fw = sb("fw", [P, 1])
        gb = sb("gb", [P, 6])
        b_zr = sb("b_zr", [P, 2])
        b_att1 = sb("b_att1", [P, 1])
        b_att2 = sb("b_att2", [H, 1])
        b_att3 = sb("b_att3", [P, 1])
        b_au = sb("b_au", [P, 3])
        b_d1 = sb("b_d1", [P, 2])
        b_d2 = sb("b_d2", [P, 1])
        b_f = sb("b_f", [1, 1])
        bn_in = sb("bn_in", [P, 8])
        bn_t = sb("bn_t", [P, 6, 2])
        x32 = sb("x32", [P, NC, CH])
        x_hi = sb("x_hi", [P, NC, CH], F16)
        x_lo = sb("x_lo", [P, NC, CH], F16)
        h32 = sb("h32", [P, NC, CH])
        h_hi = sb("h_hi", [P, NC, CH], F16)
        h_lo = sb("h_lo", [P, NC, CH], F16)
        g32 = sb("g32", [P, NC, CH])
        g_hi = sb("g_hi", [P, NC, CH], F16)
        g_lo = sb("g_lo", [P, NC, CH], F16)
        news = sb("news", [P, NC, CH])
        news_bn = sb("news_bn", [P, NC, CH])
        c_news = sb("c_news", [P, NC, CH])
        score = sb("score", [P, NC, CH])
        r = sb("r", [P, 2, CH])
        z = sb("z", [P, 2, CH])
        t = sb("t", [P, 2, CH])
        hc = sb("hc", [P, 2, CH])
        d = sb("d", [P, CH])
        hn = sb("hn", [P, 2, CH])
        hn_hi = sb("hn_hi", [P, 2, CH], F16)
        hn_lo = sb("hn_lo", [P, 2, CH], F16)
        a1p = sb("a1p", [P, 2, CH])
        a1_hi = sb("a1_hi", [P, 2, CH], F16)
        a1_lo = sb("a1_lo", [P, 2, CH], F16)
        a2l = sb("a2l", [H, 2, CH])
        a2p = sb("a2p", [H, 2, CH])
        a2 = sb("a2", [P, 2, CH], F16)
        gr = sb("gr", [P, 2, CH])
        gu = sb("gu", [P, 2, CH])
        gt = sb("gt", [P, 2, CH])
        gc = sb("gc", [P, 2, CH])
        gus = sb("gus", [P, 2, CH])
        gd = sb("gd", [P, CH])
        g_bn = sb("g_bn", [P, NC, CH])
        y1p = sb("y1p", [P, 2, CH])
        y1 = sb("y1", [P, 2, CH])
        y2p = sb("y2p", [P, 2, CH])
        y2 = sb("y2", [P, 2, CH])
        y = sb("y", [1, NB])
        ps = ctx.enter_context(nc.psum_tensor("ps", [P, 8, CH], F32))

        w_landed = [sem(f"w_landed{k}") for k in range(4)]
        news_landed = sem("news_landed")
        x_landed = [sem(f"x_landed{c}") for c in range(NC)]
        zeroed = sem("zeroed")
        prep = sem("prep")
        w_ready = sem("w_ready")
        sqrt_done, bn_ready = sem("sqrt_done"), sem("bn_ready")
        news_pe, c_ready = sem("news_pe"), sem("c_ready")
        xhi_ready, xlo_ready = sem("xhi_ready"), sem("xlo_ready")
        r_pe, hh_pe, z_pe, xh_pe = sem("r_pe"), sem("hh_pe"), sem("z_pe"), sem("xh_pe")
        r_ready, z_ready, hc_ready = sem("r_ready"), sem("z_ready"), sem("hc_ready")
        t1_ready, t2_ready = sem("t1_ready"), sem("t2_ready")
        d_ready, e_ready, h_ready = sem("d_ready"), sem("e_ready"), sem("h_ready")
        hhi_ready, hlo_ready = sem("hhi_ready"), sem("hlo_ready")
        hn_ready, hnhi_ready, hnlo_ready = sem("hn_ready"), sem("hnhi_ready"), sem("hnlo_ready")
        a1_pe, a1p_ready, a1hi_ready, a1lo_ready = sem("a1_pe"), sem("a1p_ready"), sem("a1hi_ready"), sem("a1lo_ready")
        a2_pe, a2l_ready, a2p_ready = sem("a2_pe"), sem("a2l_ready"), sem("a2p_ready")
        a2hi_ready, a2lo_ready = sem("a2hi_ready"), sem("a2lo_ready")
        score_pe, score_ready = sem("score_pe"), sem("score_ready")
        gr_pe, ghh_pe, gxh_pe, gu_pe = sem("gr_pe"), sem("ghh_pe"), sem("gxh_pe"), sem("gu_pe")
        gr_ready, gu_ready, gc_ready = sem("gr_ready"), sem("gu_ready"), sem("gc_ready")
        gt1_ready, gt2_ready, gus_ready = sem("gt1_ready"), sem("gt2_ready"), sem("gus_ready")
        gd_ready, ge_ready, g_ready = sem("gd_ready"), sem("ge_ready"), sem("g_ready")
        ghi_ready, glo_ready = sem("ghi_ready"), sem("glo_ready")
        gbn_ready = sem("gbn_ready")
        d1_pe, y1p_ready, y1_ready = sem("d1_pe"), sem("y1p_ready"), sem("y1_ready")
        d2_pe, y2p_ready, y2_ready = sem("d2_pe"), sem("y2p_ready"), sem("y2_ready")
        f_pe, y_ready, y_stored = sem("f_pe"), sem("y_ready"), sem("y_stored")

        def gate(k, w):
            return w[:, k * P:(k + 1) * P]

        loads = [
            [(w32[:, W_R, :], gate(1, gru_W)), (w32[:, W_Z, :], gate(0, gru_W)), (w32[:, W_H, :], gate(2, gru_W)),
             (gb[:, :], gru_b)],
            [(w32[:, U_R, :], gate(1, gru_U)), (w32[:, U_Z, :], gate(0, gru_U)), (w32[:, U_H, :], gate(2, gru_U))],
            [(w1[:, :, :], att_W1[0:3 * P, :].rearrange("(k p) m -> p k m", p=P)),
             (w32[:, A_HN, :], att_W1[3 * P:4 * P, :]), (w32[:, A_2, 0:H], att_W2), (w32[:, A_2, H:P], att_W2),
             (w3[0:H, :], att_W3), (w3[H:P, :], att_W3),
             (b_att1[:, :], att_b1), (b_att2[:, :], att_b2), (b_att3[:, :], att_b3)],
            [(w32[:, GW_R, :], au_Wr), (w32[:, GW_U, :], au_Wu), (w32[:, GW_C, :], au_Wc),
             (w32[:, GU_R, :], au_Ur), (w32[:, GU_U, :], au_Uu), (w32[:, GU_C, :], au_Uc),
             (b_au[:, 0:1], au_bu), (b_au[:, 1:2], au_br), (b_au[:, 2:3], au_bc),
             (bn_in[:, :], bn), (dw1[:, :, :], d_W1.rearrange("(k p) m -> p k m", p=P)),
             (dw2[:, :, :], d_W2.rearrange("(k p) m -> p k m", p=P)),
             (fw[:, :], f_W), (b_d1[:, :], d_b1), (b_d2[:, :], d_b2), (b_f[:, :], f_b)],
        ]

        def load(eng, k, lo, hi):
            for dst, src in loads[k][lo:hi]:
                eng.dma_start(dst, src).then_inc(w_landed[k], 16)

        def landed(k):
            return 16 * len(loads[k])

        PREP_VAR, PREP_ATT = 3, 14

        block = ctx.enter_context(nc.Block())

        @block.sync
        def _(sp):
            def load_x(step, c):
                return sp.dma_start(x32[:, c, :], xs[step, :, c * CH:(c + 1) * CH])

            load(sp, 0, 0, 2)
            load_x(0, 0).then_inc(x_landed[0], 16)
            load_x(0, 1).then_inc(x_landed[1], 16)
            sp.dma_start(news[:, :, :], xs[T, :, :].rearrange("p (c n) -> p c n", c=NC)).then_inc(news_landed, 16)
            load_x(0, 2).then_inc(x_landed[2], 16)
            load_x(0, 3).then_inc(x_landed[3], 16)
            load(sp, 1, 0, 3)
            load(sp, 3, 0, len(loads[3]))
            with sp.Fori(1, T) as step:
                for c in range(NC):
                    sp.wait_ge(xlo_ready, 4 * step + (c - 3))
                    load_x(step, c).then_inc(x_landed[c], 16)
            sp.wait_ge(y_ready, NC)
            sp.dma_start(out, y[:, :]).then_inc(y_stored, 16)
            sp.wait_ge(y_stored, 16)

        @block.gpsimd
        def _(pool):
            g = nc.gpsimd
            g.memset(h32[:, :, :], 0.0).then_inc(zeroed, 1)
            g.memset(ones[:, :], 1.0).then_inc(zeroed, 1)

            def slot(s0, off):
                low = off + (s0 if isinstance(s0, int) else LOOP_LO)

                def at(lag):
                    return s0 + (off - lag + 1)

                if has(low + 2):
                    c = (low + 2) % NC
                    pool.wait_ge(xhi_ready, at(-2))
                    g.tensor_tensor(x_lo[:, c, :], x32[:, c, :], x_hi[:, c, :], ALU.subtract).then_inc(xlo_ready, 1)
                if has(low - 4):
                    c, k = (low - 4) % NC, (low - 4) % 2
                    pool.wait_ge(score_ready, at(4))
                    pool.wait_ge(gu_ready, at(4))
                    g.tensor_tensor(gus[:, k, :], gu[:, k, :], score[:, c, :], ALU.mult).then_inc(gus_ready, 1)
                if has(low - 2):
                    k = (low - 2) % 2
                    pool.wait_ge(hnhi_ready, at(2))
                    g.tensor_tensor(hn_lo[:, k, :], hn[:, k, :], hn_hi[:, k, :], ALU.subtract).then_inc(hnlo_ready, 1)
                if has(low - 1):
                    c, k = (low - 1) % NC, (low - 1) % 2
                    if low - 1 == 0:
                        pool.wait_ge(news_landed, 16)
                    pool.wait_ge(h_ready, at(1))
                    g.tensor_tensor(hn[:, k, :], h32[:, c, :], news[:, c, :], ALU.mult).then_inc(hn_ready, 1)
                    pool.wait_ge(hhi_ready, at(1))
                    g.tensor_tensor(h_lo[:, c, :], h32[:, c, :], h_hi[:, c, :], ALU.subtract).then_inc(hlo_ready, 1)

            for s in range(FIRST, LOOP_LO):
                slot(s - s % NC, s % NC)
                if s == FIRST:
                    g.memset(g32[:, :, :], 0.0).then_inc(zeroed, 1)
            with pool.Fori(LOOP_LO, LOOP_HI, NC) as s0:
                for off in range(NC):
                    slot(s0, off)
            for s in range(LOOP_HI, LAST):
                slot(s - s % NC, s % NC)

        @block.scalar
        def _(act):
            a = nc.scalar
            load(act, 0, 2, 4)
            load(act, 2, 0, len(loads[2]))

            def slot(s0, off):
                low = off + (s0 if isinstance(s0, int) else LOOP_LO)

                def at(lag):
                    return s0 + (off - lag + 1)

                def late(lag):
                    return s0 + (off - lag + 1 - NC)

                if has(low - 3):
                    k = (low - 3) % 2
                    act.wait_ge(a1p_ready, at(3))
                    a.activation(a1_hi[:, k, :], a1p[:, k, :], ACT.Relu).then_inc(a1hi_ready, 1)
                if has(low - 1):
                    k = (low - 1) % 2
                    act.wait_ge(t2_ready, at(1))
                    a.activation(hc[:, k, :], t[:, k, :], ACT.Tanh, bias=gb[:, 2:3]).then_inc(hc_ready, 1)
                if has(low - 2):
                    k = (low - 2) % 2
                    act.wait_ge(hn_ready, at(2))
                    a.activation(hn_hi[:, k, :], hn[:, k, :], ACT.Copy).then_inc(hnhi_ready, 1)
                if has(low - 4):
                    act.wait_ge(gu_pe, at(4))
                    a.activation(gu[:, (low - 4) % 2, :], ps[:, B_GU, :], ACT.Sigmoid, bias=b_au[:, 0:1]).then_inc(gu_ready, 1)
                if has(low - 3):
                    act.wait_ge(a2_pe, at(3))
                    a.activation(a2l[:, (low - 3) % 2, :], ps[H:P, B_A2, :], ACT.Copy).then_inc(a2l_ready, 1)
                if has(low):
                    if low == 0:
                        act.wait_ge(w_ready, 1)
                    act.wait_ge(r_pe, at(0))
                    a.activation(r[:, low % 2, :], ps[:, B_R, :], ACT.Sigmoid, bias=b_zr[:, 1:2]).then_inc(r_ready, 1)
                if has(low - 4):
                    k = (low - 4) % 2
                    if low - 4 < NC:
                        act.wait_ge(gxh_pe, at(4))
                        a.activation(gc[:, k, :], ps[:, B_GXH, :], ACT.Tanh, bias=b_au[:, 2:3]).then_inc(gc_ready, 1)
                    else:
                        act.wait_ge(gt2_ready, late(4))
                        a.activation(gc[:, k, :], gt[:, k, :], ACT.Tanh, bias=b_au[:, 2:3]).then_inc(gc_ready, 1)
                if has(low - 3):
                    k = (low - 3) % 2
                    act.wait_ge(a2p_ready, at(3))
                    a.activation(a2[0:H, k, :], a2p[:, k, :], ACT.Relu).then_inc(a2hi_ready, 1)
                if has(low - 3) and low - 3 >= NC:
                    act.wait_ge(gr_pe, late(3))
                    a.activation(gr[:, (low - 3) % 2, :], ps[:, B_GR, :], ACT.Sigmoid, bias=b_au[:, 1:2]).then_inc(gr_ready, 1)
                if has(low):
                    act.wait_ge(z_pe, at(0))
                    a.activation(z[:, low % 2, :], ps[:, B_Z, :], ACT.Sigmoid, bias=b_zr[:, 0:1]).then_inc(z_ready, 1)
                if has(low - 1):
                    c = (low - 1) % NC
                    act.wait_ge(h_ready, at(1))
                    a.activation(h_hi[:, c, :], h32[:, c, :], ACT.Copy).then_inc(hhi_ready, 1)
                if has(low - 5) and has(low - 5 + NC):
                    c = (low - 5) % NC
                    act.wait_ge(g_ready, at(5))
                    a.activation(g_hi[:, c, :], g32[:, c, :], ACT.Copy).then_inc(ghi_ready, 1)
                if has(low + 3):
                    c = (low + 3) % NC
                    act.wait_ge(x_landed[c], 4 * (s0 + (off + 3 - c)) + 16)
                    if low - 1 >= 0:
                        act.wait_ge(xh_pe, at(1))
                    a.activation(x_hi[:, c, :], x32[:, c, :], ACT.Copy).then_inc(xhi_ready, 1)
                if has(low - 3):
                    act.wait_ge(score_pe, at(3))
                    a.activation(score[:, (low - 3) % NC, :], ps[:, B_SCORE, :], ACT.Sigmoid,
                                 bias=b_att3[:, :]).then_inc(score_ready, 1)

            for s in range(FIRST, LOOP_LO):
                slot(s - s % NC, s % NC)
                if s == 0:
                    act.wait_ge(prep, PREP_VAR)
                    a.activation(bn_t[:, 1, :], bn_t[:, 0, :], ACT.Sqrt).then_inc(sqrt_done, 1)
            with act.Fori(LOOP_LO, LOOP_HI, NC) as s0:
                for off in range(NC):
                    slot(s0, off)
            for s in range(LOOP_HI, LAST):
                slot(s - s % NC, s % NC)
                c = s - HEAD
                if 0 <= c - 1 < NC:
                    act.wait_ge(d2_pe, c)
                    a.activation(y2p[:, c % 2, :], ps[:, B_D2, :], ACT.Identity, bias=b_d2[:, :]).then_inc(y2p_ready, 1)
                if 0 <= c < NC:
                    for m in range(2):
                        act.wait_ge(d1_pe, 2 * c + m + 1)
                        a.activation(y1p[:, m, :], ps[:, B_D1[m], :], ACT.Identity, bias=b_d1[:, m:m + 1]).then_inc(y1p_ready, 1)
                if 0 <= c - 2 < NC:
                    act.wait_ge(f_pe, c - 1)
                    a.activation(y[0:1, (c - 2) * CH:(c - 1) * CH], ps[0:1, B_F, :], ACT.Sigmoid,
                                 bias=b_f[:, :]).then_inc(y_ready, 1)

        @block.vector
        def _(dve):
            v = nc.vector

            def split(lo, hi, done):
                dve.wait_ge(prep, done)
                v.tensor_copy(w_hi[:, lo:hi, :], w32[:, lo:hi, :]).then_inc(prep, 1)
                dve.wait_ge(prep, done + 1)
                v.tensor_tensor(w_lo[:, lo:hi, :], w32[:, lo:hi, :], w_hi[:, lo:hi, :], ALU.subtract).then_inc(w_ready, 1)

            def prepare_gru():
                dve.wait_ge(w_landed[0], landed(0))
                v.tensor_tensor(b_zr[:, :], gb[:, 0:2], gb[:, 3:5], ALU.add).then_inc(prep, 1)
                split(W_R, W_H + 1, 1)
                dve.wait_ge(zeroed, 2)

            def prepare_att():
                dve.wait_ge(w_landed[3], landed(3))
                v.tensor_scalar(bn_t[:, 0, :], bn_in[:, 6:8], BN_EPS, None, ALU.add).then_inc(prep, 1)
                dve.wait_ge(w_landed[2], landed(2))
                v.tensor_tensor(w1_news[:, :], w1[:, 1, :], w1[:, 2, :], ALU.add).then_inc(prep, 1)
                v.tensor_tensor(w32[:, A_HS, :], w1[:, 0, :], w1[:, 1, :], ALU.subtract).then_inc(prep, 1)
                v.tensor_scalar(w3_rep[:, :], ones[:, :], w3[:, 0:1], None, ALU.mult).then_inc(prep, 1)
                v.memset(w3_lo[:, :], 0.0).then_inc(prep, 1)
                v.memset(w2_sum[:, 1, :], 0.0).then_inc(prep, 1)
                split(A_HS, A_2 + 1, 8)
                v.tensor_copy(w3_hi[:, :], w3_rep[:, :]).then_inc(prep, 1)
                dve.wait_ge(prep, 10)
                v.tensor_tensor(w3_lo[0:H, :], w3_rep[0:H, :], w3_hi[0:H, :], ALU.subtract).then_inc(prep, 1)
                dve.wait_ge(w_ready, 2)
                for k, part in ((0, w_hi[:, A_2, 0:H]), (1, w_hi[:, A_2, 0:H])):
                    v.tensor_copy(w2_sum[:, k, 0:H], part).then_inc(prep, 1)
                v.tensor_copy(w2_sum[:, 0, H:P], w_lo[:, A_2, H:P]).then_inc(prep, 1)
                dve.wait_ge(prep, PREP_ATT)

            def prepare_state():
                dve.wait_ge(w_landed[1], landed(1))
                split(U_R, U_H + 1, PREP_ATT)

            def prepare_gated():
                split(GW_R, GU_C + 1, PREP_ATT + 1)

            def prepare_bn():
                dve.wait_ge(sqrt_done, 1)
                v.reciprocal(bn_t[:, 2, :], bn_t[:, 1, :]).then_inc(bn_ready, 1)
                dve.wait_ge(bn_ready, 1)
                v.tensor_tensor(bn_t[:, 3, :], bn_t[:, 2, :], bn_t[:, 2, :], ALU.mult).then_inc(bn_ready, 1)
                dve.wait_ge(bn_ready, 2)
                v.tensor_tensor(bn_t[:, 3, :], bn_t[:, 3, :], bn_t[:, 0, :], ALU.mult).then_inc(bn_ready, 1)
                dve.wait_ge(bn_ready, 3)
                v.tensor_scalar(bn_t[:, 3, :], bn_t[:, 3, :], -0.5, 1.5, ALU.mult, ALU.add).then_inc(bn_ready, 1)
                dve.wait_ge(bn_ready, 4)
                v.tensor_tensor(bn_t[:, 3, :], bn_t[:, 3, :], bn_t[:, 2, :], ALU.mult).then_inc(bn_ready, 1)
                dve.wait_ge(bn_ready, 5)
                v.tensor_tensor(bn_t[:, 4, :], bn_t[:, 3, :], bn_in[:, 0:2], ALU.mult).then_inc(bn_ready, 1)
                dve.wait_ge(bn_ready, 6)
                v.tensor_tensor(bn_t[:, 3, :], bn_in[:, 4:6], bn_t[:, 4, :], ALU.mult).then_inc(bn_ready, 1)
                dve.wait_ge(bn_ready, 7)
                v.tensor_tensor(bn_t[:, 5, :], bn_in[:, 2:4], bn_t[:, 3, :], ALU.subtract).then_inc(bn_ready, 1)
                dve.wait_ge(bn_ready, 8)
                v.tensor_scalar(news_bn[:, :, :], news[:, :, :], bn_t[:, 4, 1:2], bn_t[:, 5, 1:2],
                                ALU.mult, ALU.add).then_inc(bn_ready, 1)

            def slot(s0, off):
                low = off + (s0 if isinstance(s0, int) else LOOP_LO)

                def at(lag):
                    return s0 + (off - lag + 1)

                def late(lag):
                    return s0 + (off - lag + 1 - NC)

                if has(low - 5):
                    dve.wait_ge(gus_ready, at(5))
                    dve.wait_ge(gd_ready, at(5))
                    v.tensor_tensor(gd[:, :], gd[:, :], gus[:, (low - 5) % 2, :], ALU.mult).then_inc(ge_ready, 1)
                if has(low - 3):
                    c = (low - 3) % NC
                    dve.wait_ge(a1_pe, at(3))
                    if low - 3 < NC:
                        dve.wait_ge(c_ready, low - 3 + 1)
                    v.tensor_tensor(a1p[:, (low - 3) % 2, :], c_news[:, c, :], ps[:, B_A1, :], ALU.add).then_inc(a1p_ready, 1)
                if has(low - 1):
                    k = (low - 1) % 2
                    dve.wait_ge(xh_pe, at(1))
                    dve.wait_ge(t1_ready, at(1))
                    v.tensor_tensor(t[:, k, :], t[:, k, :], ps[:, B_XH, :], ALU.add).then_inc(t2_ready, 1)
                if has(low - 5):
                    c = (low - 5) % NC
                    dve.wait_ge(ge_ready, at(5))
                    v.tensor_tensor(g32[:, c, :], g32[:, c, :], gd[:, :], ALU.add).then_inc(g_ready, 1)
                if has(low - 3):
                    k = (low - 3) % 2
                    dve.wait_ge(a1hi_ready, at(3))
                    v.scalar_tensor_tensor(out=a1_lo[:, k, :], in0=a1p[:, k, :], scalar=0.0,
                                           in1=a1_hi[:, k, :], op0=ALU.max, op1=ALU.subtract).then_inc(a1lo_ready, 1)
                if has(low - 4) and low - 4 >= NC:
                    k = (low - 4) % 2
                    dve.wait_ge(ghh_pe, late(4))
                    dve.wait_ge(gr_ready, late(4))
                    v.tensor_tensor(gt[:, k, :], gr[:, k, :], ps[:, B_GHH, :], ALU.mult).then_inc(gt1_ready, 1)
                if has(low - 1):
                    dve.wait_ge(hc_ready, at(1))
                    v.tensor_tensor(d[:, :], h32[:, (low - 1) % NC, :], hc[:, (low - 1) % 2, :], ALU.subtract).then_inc(d_ready, 1)
                if has(low - 6) and has(low - 6 + NC):
                    c = (low - 6) % NC
                    dve.wait_ge(ghi_ready, at(6))
                    v.tensor_tensor(g_lo[:, c, :], g32[:, c, :], g_hi[:, c, :], ALU.subtract).then_inc(glo_ready, 1)
                if has(low - 4) and low - 4 >= NC:
                    k = (low - 4) % 2
                    dve.wait_ge(gxh_pe, at(4))
                    dve.wait_ge(gt1_ready, late(4))
                    v.tensor_tensor(gt[:, k, :], gt[:, k, :], ps[:, B_GXH, :], ALU.add).then_inc(gt2_ready, 1)
                if has(low - 1):
                    dve.wait_ge(z_ready, at(1))
                    dve.wait_ge(d_ready, at(1))
                    v.tensor_tensor(d[:, :], d[:, :], z[:, (low - 1) % 2, :], ALU.mult).then_inc(e_ready, 1)
                if has(low - 3):
                    k = (low - 3) % 2
                    dve.wait_ge(a2l_ready, at(3))
                    v.scalar_tensor_tensor(out=a2p[:, k, :], in0=ps[0:H, B_A2, :], scalar=b_att2[:, 0:1],
                                           in1=a2l[:, k, :], op0=ALU.add, op1=ALU.add).then_inc(a2p_ready, 1)
                if has(low - 1):
                    dve.wait_ge(e_ready, at(1))
                    v.tensor_tensor(h32[:, (low - 1) % NC, :], hc[:, (low - 1) % 2, :], d[:, :], ALU.add).then_inc(h_ready, 1)
                if has(low - 4):
                    if low - 4 == 0:
                        dve.wait_ge(zeroed, 3)
                    dve.wait_ge(gc_ready, at(4))
                    v.tensor_tensor(gd[:, :], gc[:, (low - 4) % 2, :], g32[:, (low - 4) % NC, :], ALU.subtract).then_inc(gd_ready, 1)
                if has(low - 3):
                    k = (low - 3) % 2
                    dve.wait_ge(a2hi_ready, at(3))
                    v.scalar_tensor_tensor(out=a2[H:P, k, :], in0=a2p[:, k, :], scalar=0.0,
                                           in1=a2[0:H, k, :], op0=ALU.max, op1=ALU.subtract).then_inc(a2lo_ready, 1)
                if has(low):
                    dve.wait_ge(r_ready, at(0))
                    if low < NC:
                        v.tensor_scalar(t[:, low % 2, :], r[:, low % 2, :], gb[:, 5:6], None, ALU.mult).then_inc(t1_ready, 1)
                    else:
                        dve.wait_ge(hh_pe, late(0))
                        v.scalar_tensor_tensor(out=t[:, low % 2, :], in0=ps[:, B_HH, :], scalar=gb[:, 5:6],
                                               in1=r[:, low % 2, :], op0=ALU.add, op1=ALU.mult).then_inc(t1_ready, 1)

            prepare_gru()
            for s in range(0, LOOP_LO):
                slot(s - s % NC, s % NC)
                if s < NC:
                    if s == 0:
                        prepare_att()
                    dve.wait_ge(news_pe, s + 1)
                    v.tensor_scalar(c_news[:, s, :], ps[:, B_NEWS[s % 2], :], b_att1[:, 0:1], None, ALU.add).then_inc(c_ready, 1)
                if s == 1:
                    prepare_state()
                if s == 2:
                    prepare_gated()
                if s == NC + 2:
                    prepare_bn()
            with dve.Fori(LOOP_LO, LOOP_HI, NC) as s0:
                for off in range(NC):
                    slot(s0, off)
            for s in range(LOOP_HI, LAST):
                slot(s - s % NC, s % NC)
                c = s - HEAD
                if 0 <= c + 1 < NC:
                    dve.wait_ge(bn_ready, 9)
                    dve.wait_ge(g_ready, ITEMS - NC + c + 2)
                    v.tensor_scalar(g_bn[:, c + 1, :], g32[:, c + 1, :], bn_t[:, 4, 0:1], bn_t[:, 5, 0:1],
                                    ALU.mult, ALU.add).then_inc(gbn_ready, 1)
                if 0 <= c - 1 < NC:
                    dve.wait_ge(y2p_ready, c)
                    v.scalar_tensor_tensor(out=y2[:, c % 2, :], in0=y2p[:, c % 2, :], scalar=LEAKY,
                                           in1=y2p[:, c % 2, :], op0=ALU.mult, op1=ALU.max).then_inc(y2_ready, 1)
                if 0 <= c < NC:
                    for m in range(2):
                        dve.wait_ge(y1p_ready, 2 * c + m + 1)
                        v.scalar_tensor_tensor(out=y1[:, m, :], in0=y1p[:, m, :], scalar=LEAKY,
                                               in1=y1p[:, m, :], op0=ALU.mult, op1=ALU.max).then_inc(y1_ready, 1)

        @block.tensor
        def _(pe):
            m = nc.tensor

            def split_product(bank, w, hi, lo, start, stop):
                m.matmul(ps[:, bank, :], w_hi[:, w, :], hi, start=start, stop=False)
                m.matmul(ps[:, bank, :], w_hi[:, w, :], lo, start=False, stop=False)
                return m.matmul(ps[:, bank, :], w_lo[:, w, :], hi, start=False, stop=stop)

            def slot(s0, off):
                low = off + (s0 if isinstance(s0, int) else LOOP_LO)

                def at(lag):
                    return s0 + (off - lag + 1)

                def late(lag):
                    return s0 + (off - lag + 1 - NC)

                def parts(hi, lo, n, lag):
                    k = (low - lag) % n
                    return hi[:, k, :], lo[:, k, :]

                if has(low - 4):
                    h, g = parts(h_hi, h_lo, NC, 4), parts(g_hi, g_lo, NC, 4)
                    first = low - 4 < NC
                    if low - 4 == 0:
                        pe.wait_ge(w_ready, 4)
                    pe.wait_ge(a2p_ready, at(4))
                    if first:
                        split_product(B_GU, GW_U, *h, start=True, stop=True).then_inc(gu_pe, 1)
                    else:
                        split_product(B_GU, GW_U, *h, start=True, stop=False)
                        split_product(B_GU, GU_U, *g, start=False, stop=True).then_inc(gu_pe, 1)
                    if low - 4 == NC:
                        pe.wait_ge(gc_ready, NC)
                    elif low - 4 > NC:
                        pe.wait_ge(gt2_ready, late(5))
                    elif low - 4 > 0:
                        pe.wait_ge(gc_ready, at(5))
                    split_product(B_GXH, GW_C, *h, start=True, stop=True).then_inc(gxh_pe, 1)
                if has(low):
                    x, h = parts(x_hi, x_lo, NC, 0), parts(h_hi, h_lo, NC, 0)
                    if low == 0:
                        pe.wait_ge(w_ready, 1)
                    if low == NC:
                        pe.wait_ge(w_ready, 3)
                    pe.wait_ge(xlo_ready, at(0))
                    if low >= NC:
                        pe.wait_ge(hlo_ready, at(NC))
                        pe.wait_ge(t1_ready, at(1))
                        split_product(B_HH, U_H, *h, start=True, stop=True).then_inc(hh_pe, 1)
                    if low >= 1:
                        pe.wait_ge(t2_ready, at(1))
                    if low < NC:
                        split_product(B_R, W_R, *x, start=True, stop=True).then_inc(r_pe, 1)
                    else:
                        split_product(B_R, W_R, *x, start=True, stop=False)
                        split_product(B_R, U_R, *h, start=False, stop=True).then_inc(r_pe, 1)
                if has(low - 3):
                    a1 = parts(a1_hi, a1_lo, 2, 3)
                    if low - 4 >= 0:
                        pe.wait_ge(gu_ready, at(4))
                    pe.wait_ge(a1lo_ready, at(3))
                    m.matmul(ps[:, B_A2, :], w2_sum[:, 0, :], a1[0], start=True, stop=False)
                    m.matmul(ps[:, B_A2, :], w2_sum[:, 1, :], a1[1], start=False, stop=True).then_inc(a2_pe, 1)
                if has(low):
                    if low >= 4:
                        pe.wait_ge(score_ready, at(4))
                    elif low >= 1:
                        pe.wait_ge(z_ready, at(1))
                    if low < NC:
                        split_product(B_Z, W_Z, *x, start=True, stop=True).then_inc(z_pe, 1)
                    else:
                        split_product(B_Z, W_Z, *x, start=True, stop=False)
                        split_product(B_Z, U_Z, *h, start=False, stop=True).then_inc(z_pe, 1)
                if has(low - 3) and low - 3 >= NC:
                    if low - 3 > NC:
                        pe.wait_ge(gr_ready, late(4))
                    split_product(B_GR, GW_R, *parts(h_hi, h_lo, NC, 3), start=True, stop=False)
                    g = parts(g_hi, g_lo, NC, 3)
                    pe.wait_ge(glo_ready, at(3 + NC))
                    split_product(B_GR, GU_R, *g, start=False, stop=True).then_inc(gr_pe, 1)
                    if low - 3 > NC:
                        pe.wait_ge(gt1_ready, late(4))
                    split_product(B_GHH, GU_C, *g, start=True, stop=True).then_inc(ghh_pe, 1)
                if has(low - 2):
                    if low - 2 >= 1:
                        pe.wait_ge(a1p_ready, at(3))
                    pe.wait_ge(hlo_ready, at(2))
                    split_product(B_A1, A_HS, *parts(h_hi, h_lo, NC, 2), start=True, stop=False)
                    pe.wait_ge(hnlo_ready, at(2))
                    split_product(B_A1, A_HN, *parts(hn_hi, hn_lo, 2, 2), start=False, stop=True).then_inc(a1_pe, 1)
                if has(low - 3):
                    a2k = a2[:, (low - 3) % 2, :]
                    pe.wait_ge(a2lo_ready, at(3))
                    if has(low):
                        pe.wait_ge(z_ready, at(0))
                    else:
                        pe.wait_ge(score_ready, at(4))
                    m.matmul(ps[:, B_SCORE, :], w3_hi[:, :], a2k, start=True, stop=False)
                    m.matmul(ps[:, B_SCORE, :], w3_lo[:, :], a2k, start=False, stop=True).then_inc(score_pe, 1)
                if has(low):
                    pe.wait_ge(r_ready, at(0))
                    split_product(B_XH, W_H, *x, start=True, stop=True).then_inc(xh_pe, 1)

            for s in range(0, LOOP_LO):
                slot(s - s % NC, s % NC)
                if s < NC:
                    if s == 0:
                        pe.wait_ge(w_ready, 2)
                        pe.wait_ge(prep, PREP_ATT)
                        pe.wait_ge(news_landed, 16)
                    if s >= 2:
                        pe.wait_ge(c_ready, s - 1)
                    m.matmul(ps[:, B_NEWS[s % 2], :], w1_news[:, :], news[:, s, :], start=True, stop=True).then_inc(news_pe, 1)
            with pe.Fori(LOOP_LO, LOOP_HI, NC) as s0:
                for off in range(NC):
                    slot(s0, off)
            for s in range(LOOP_HI, LAST):
                slot(s - s % NC, s % NC)
                c = s - HEAD
                if 0 <= c - 1 < NC:
                    if c == 1:
                        pe.wait_ge(score_ready, ITEMS)
                    else:
                        pe.wait_ge(y2p_ready, c - 1)
                    pe.wait_ge(y1_ready, 2 * c)
                    m.matmul(ps[:, B_D2, :], dw2[:, 0, :], y1[:, 0, :], start=True, stop=False)
                    m.matmul(ps[:, B_D2, :], dw2[:, 1, :], y1[:, 1, :], start=False, stop=True).then_inc(d2_pe, 1)
                if 0 <= c < NC:
                    for k in range(2):
                        if c == 0:
                            pe.wait_ge(t2_ready, ITEMS)
                        else:
                            pe.wait_ge(y1p_ready, 2 * c - 1 + k)
                        m.matmul(ps[:, B_D1[k], :], dw1[:, 1, k * P:(k + 1) * P], news_bn[:, c, :], start=True, stop=False)
                    pe.wait_ge(gbn_ready, c + 1)
                    for k in range(2):
                        m.matmul(ps[:, B_D1[k], :], dw1[:, 0, k * P:(k + 1) * P], g_bn[:, c, :],
                                 start=False, stop=True).then_inc(d1_pe, 1)
                if 0 <= c - 2 < NC:
                    if c > 2:
                        pe.wait_ge(y_ready, c - 2)
                    pe.wait_ge(y2_ready, c - 1)
                    m.matmul(ps[0:1, B_F, :], fw[:, :], y2[:, (c - 1) % 2, :], start=True, stop=True).then_inc(f_pe, 1)


def kernel(**inputs):
    import numpy as np
    import concourse.bacc as bacc
    from concourse.bass_utils import run_bass_kernel_spmd

    w = {k[len("L0_rec_"):]: np.asarray(v) for k, v in inputs.items() if k != "r_inputs"}
    x = np.asarray(inputs["r_inputs"])

    def columns(v):
        return np.ascontiguousarray(v.reshape(-1, P).T)

    bn = np.concatenate([columns(w[k]) for k in ("bn_gamma", "bn_beta", "bn_mean", "bn_var")], axis=1)
    arrays = {
        "xs": np.ascontiguousarray(x.transpose(1, 2, 0)),
        "gru_W": w["gru_W"], "gru_U": w["gru_U"], "gru_b": columns(w["gru_b"]),
        "att_W1": w["att_W1"], "att_b1": w["att_b1"].reshape(P, 1), "att_W2": w["att_W2"],
        "att_b2": w["att_b2"].reshape(H, 1), "att_W3": w["att_W3"],
        "att_b3": np.ascontiguousarray(np.broadcast_to(w["att_b3"].reshape(1, 1), (P, 1))),
        "au_Wu": w["au_Wu"], "au_bu": w["au_bu"].reshape(P, 1), "au_Uu": w["au_Uu"],
        "au_Wr": w["au_Wr"], "au_br": w["au_br"].reshape(P, 1), "au_Ur": w["au_Ur"],
        "au_Wc": w["au_Wc"], "au_bc": w["au_bc"].reshape(P, 1), "au_Uc": w["au_Uc"],
        "bn": bn, "d_W1": w["d_W1"], "d_b1": columns(w["d_b1"]), "d_W2": w["d_W2"],
        "d_b2": w["d_b2"].reshape(P, 1), "f_W": w["f_W"], "f_b": w["f_b"].reshape(1, 1),
    }
    nc = bacc.Bacc("TRN2", target_bir_lowering=False, num_devices=1)
    feed, args = {}, []
    for name, value in arrays.items():
        value = np.ascontiguousarray(value)
        feed[f"in_{name}"] = value
        args.append(nc.dram_tensor(f"in_{name}", value.shape, mybir.dt.from_np(value.dtype), kind="ExternalInput").ap())
    out = nc.dram_tensor("out_y", (1, x.shape[0]), F32, kind="ExternalOutput").ap()
    rec_kernel(nc, *args, out)
    result = run_bass_kernel_spmd(nc, [feed], core_ids=[0])
    return result.results[0]["out_y"].reshape(x.shape[0], 1)
```

```python
from contextlib import ExitStack

import concourse.bass as bass
from concourse import mybir

ALU = mybir.AluOpType
ACT = mybir.ActivationFunctionType
F32 = mybir.dt.float32
F16 = mybir.dt.float16
I32 = mybir.dt.int32

P = 128
H = P // 2
CH = 512
NC = 4
LEAKY = 0.0003
BN_EPS = 0.001
RSQRT_MAGIC = float(0x5F3759DF)
NEWTON = 4

B_XH, B_A1, B_HH, B_R, B_A2, B_GHH, B_Z, B_GXH = range(8)
B_SCORE, B_GR, B_GU = B_XH, B_R, B_Z
B_Z0, B_XH0 = (B_Z, B_GHH), (B_XH, B_HH)
B_NEWS = (B_GXH, B_A2, B_GXH, B_XH)
B_GU0 = B_GHH
B_D1 = ((B_HH, B_A1), (B_R, B_A2), (B_Z, B_GHH), (B_HH, B_A1))
B_D2, B_F = (B_XH, B_GXH), (B_R, B_A2)

W_Z, W_R, W_H, U_Z, U_R, U_H, A_HS, A_HN, A_2, GW_U, GW_R, GW_C, GU_U, GU_R, GU_C = range(15)
NW = 15


def columns(widths):
    at, out = 0, {}
    for name, n in widths:
        out[name] = slice(at, at + n)
        at += n
    return out, at


PACK_GRU, N_GRU = columns([("W", 3 * P), ("b", 6)])
PACK_STATE, N_STATE = columns([("U", 3 * P)])
PACK_ATT, N_ATT = columns([("W1a", P), ("W1b", P), ("W1c", P), ("W1d", P), ("W2", H), ("w3_row", H), ("w3", 1),
                           ("b1", 1), ("b2", 1), ("b3", 1)])
PACK_REST, N_REST = columns([("gated", 6 * P), ("b_gated", 3), ("gamma", 2), ("beta", 2), ("mean", 2), ("var", 2),
                             ("D1", 4 * P), ("D2", 2 * P), ("F", 1), ("b_d1", 2), ("b_d2", 1), ("b_f", 1)])


def rec_kernel(nc, xs, pack_gru, pack_state, pack_att, pack_rest, out):
    T = xs.shape[0] - 1
    NB = xs.shape[2]
    assert NB == NC * CH and xs.shape[1] == P
    ITEMS = NC * T
    LOOP_LO = 3 * NC
    LOOP_HI = ITEMS - NC
    LAST = ITEMS + 4
    AHEAD = 2

    def has(item):
        return 0 <= item < ITEMS

    with ExitStack() as ctx:
        def sb(name, shape, dt=F32):
            return ctx.enter_context(nc.sbuf_tensor(name, shape, dt))

        def sem(name):
            return ctx.enter_context(nc.semaphore(name))

        p_gru = sb("p_gru", [P, N_GRU])
        p_state = sb("p_state", [P, N_STATE])
        p_att = sb("p_att", [P, N_ATT])
        p_rest = sb("p_rest", [P, N_REST])
        w_hi = sb("w_hi", [P, NW, P], F16)
        w_lo = sb("w_lo", [P, NW, P], F16)
        w_att = sb("w_att", [P, 3, P])
        w1_news = sb("w1_news", [P, P])
        w2_sum = sb("w2_sum", [P, 2, P], F16)
        w3_abs = sb("w3_abs", [P, H])
        w3_col = sb("w3_col", [P, 4])
        w3_sign = sb("w3_sign", [P, P], F16)
        b_att2 = sb("b_att2", [P, 1])
        ones = sb("ones", [P, P])
        spare = sb("spare", [P, 1])
        b_zr = sb("b_zr", [P, 2])
        bn_t = sb("bn_t", [P, 6, 2])
        x32 = sb("x32", [P, NC, CH])
        x_hi = sb("x_hi", [P, NC, CH], F16)
        x_lo = sb("x_lo", [P, NC, CH], F16)
        h32 = sb("h32", [P, NC, CH])
        h_hi = sb("h_hi", [P, NC, CH], F16)
        h_lo = sb("h_lo", [P, NC, CH], F16)
        g32 = sb("g32", [P, NC, CH])
        g_hi = sb("g_hi", [P, NC, CH], F16)
        g_lo = sb("g_lo", [P, NC, CH], F16)
        news = sb("news", [P, NC, CH])
        news_bn = sb("news_bn", [P, NC, CH])
        c_news = sb("c_news", [P, NC, CH])
        score = sb("score", [P, NC, CH])
        r = sb("r", [P, 2, CH])
        t = sb("t", [P, 2, CH])
        hc = sb("hc", [P, 2, CH])
        d = sb("d", [P, 2, CH])
        hn = sb("hn", [P, 2, CH])
        hn_hi = sb("hn_hi", [P, 2, CH], F16)
        hn_lo = sb("hn_lo", [P, 2, CH], F16)
        a1_hi = sb("a1_hi", [P, 2, CH], F16)
        a1_lo = sb("a1_lo", [P, 2, CH], F16)
        a2l = sb("a2l", [H, 2, CH])
        a2 = sb("a2", [P, 2, CH], F16)
        gr = sb("gr", [P, 2, CH])
        gu = sb("gu", [P, 2, CH])
        gt = sb("gt", [P, 2, CH])
        gus = sb("gus", [P, 2, CH])
        g_bn = x32
        y1p = sb("y1p", [P, 2, 2, CH])
        y1 = sb("y1", [P, 2, 2, CH])
        y2p = sb("y2p", [P, 2, CH])
        y2 = sb("y2", [P, 2, CH])
        y = c_news
        ps = ctx.enter_context(nc.psum_tensor("ps", [P, 8, CH], F32))

        gru_b = p_gru[:, PACK_GRU["b"]]
        b_h, b_hs = gru_b[:, 2:3], gru_b[:, 5:6]
        b_gated = p_rest[:, PACK_REST["b_gated"]]
        dw1 = p_rest[:, PACK_REST["D1"]].rearrange("p (k m) -> p k m", k=2)
        dw2 = p_rest[:, PACK_REST["D2"]].rearrange("p (k m) -> p k m", k=2)

        gru_landed, state_landed = sem("gru_landed"), sem("state_landed")
        att_landed, rest_landed = sem("att_landed"), sem("rest_landed")
        news_landed = sem("news_landed")
        x_landed = [sem(f"x_landed{c}") for c in range(NC)]
        zeroed = sem("zeroed")
        prep = sem("prep")
        b_ready = sem("b_ready")
        w_half = sem("w_half")
        w_ready = sem("w_ready")
        bn_ready = sem("bn_ready")
        news_pe, c_ready = sem("news_pe"), sem("c_ready")
        xhi_ready, xlo_ready = sem("xhi_ready"), sem("xlo_ready")
        r_pe, hh_pe, z_pe, xh_pe = sem("r_pe"), sem("hh_pe"), sem("z_pe"), sem("xh_pe")
        r_ready, z_ready, hc_ready = sem("r_ready"), sem("z_ready"), sem("hc_ready")
        t1_ready, t2_ready = sem("t1_ready"), sem("t2_ready")
        d_ready, e_ready, h_ready = sem("d_ready"), sem("e_ready"), sem("h_ready")
        hhi_ready, hlo_ready = sem("hhi_ready"), sem("hlo_ready")
        hn_ready, hnhi_ready, hnlo_ready = sem("hn_ready"), sem("hnhi_ready"), sem("hnlo_ready")
        a1_pe, a1p_ready, a1hi_ready, a1lo_ready = sem("a1_pe"), sem("a1p_ready"), sem("a1hi_ready"), sem("a1lo_ready")
        a2_pe, a2l_ready, a2p_ready = sem("a2_pe"), sem("a2l_ready"), sem("a2p_ready")
        a2hi_ready, a2lo_ready = sem("a2hi_ready"), sem("a2lo_ready")
        score_pe, score_ready = sem("score_pe"), sem("score_ready")
        gr_pe, ghh_pe, gxh_pe, gu_pe = sem("gr_pe"), sem("ghh_pe"), sem("gxh_pe"), sem("gu_pe")
        gr_ready, gu_ready, gc_ready = sem("gr_ready"), sem("gu_ready"), sem("gc_ready")
        gt1_ready, gt2_ready, gus_ready = sem("gt1_ready"), sem("gt2_ready"), sem("gus_ready")
        gd_ready, ge_ready, g_ready = sem("gd_ready"), sem("ge_ready"), sem("g_ready")
        ghi_ready, glo_ready = sem("ghi_ready"), sem("glo_ready")
        gbn_ready = sem("gbn_ready")
        d1_pe, y1p_ready, y1_ready = sem("d1_pe"), sem("y1p_ready"), sem("y1_ready")
        d2_pe, y2p_ready, y2_ready = sem("d2_pe"), sem("y2p_ready"), sem("y2_ready")
        f_pe, y_ready, y_stored = sem("f_pe"), sem("y_ready"), sem("y_stored")

        PREP_ATT = 13


        block = ctx.enter_context(nc.Block())

        @block.sync
        def _(sp):
            def load_x(step, c):
                return sp.dma_start(x32[:, c, :], xs[step, :, c * CH:(c + 1) * CH])

            sp.dma_start(p_gru[:, :], pack_gru).then_inc(gru_landed, 16)
            for c in range(NC):
                load_x(0, c).then_inc(x_landed[c], 16)
            sp.dma_start(p_att[:, :], pack_att).then_inc(att_landed, 16)
            sp.dma_start(news[:, :, :], xs[T, :, :].rearrange("p (c n) -> p c n", c=NC)).then_inc(news_landed, 16)
            sp.dma_start(p_state[:, :], pack_state).then_inc(state_landed, 16)
            sp.dma_start(p_rest[:, :], pack_rest).then_inc(rest_landed, 16)
            with sp.Fori(1, T) as step:
                for c in range(NC):
                    sp.wait_ge(xlo_ready, 4 * step + (c - 3))
                    load_x(step, c).then_inc(x_landed[c], 16)
            sp.wait_ge(y_ready, NC)
            sp.dma_start(out, y[0:1, :, :].rearrange("p c n -> p (c n)")).then_inc(y_stored, 16)
            sp.wait_ge(y_stored, 16)

        @block.gpsimd
        def _(pool):
            g = nc.gpsimd
            g.memset(ones[:, :], 1.0).then_inc(zeroed, 1)
            g.memset(g32[:, :, :], 0.0).then_inc(zeroed, 1)

            def state_news(item, count):
                c, k = item % NC, item % 2
                if item == 0:
                    pool.wait_ge(news_landed, 16)
                pool.wait_ge(h_ready, count)
                g.tensor_tensor(hn[:, k, :], h32[:, c, :], news[:, c, :], ALU.mult).then_inc(hn_ready, 1)

            def state_news_low(item, count):
                k = item % 2
                pool.wait_ge(hnhi_ready, count)
                g.tensor_tensor(hn_lo[:, k, :], hn[:, k, :], hn_hi[:, k, :], ALU.subtract).then_inc(hnlo_ready, 1)

            def state_low(item, count):
                c = item % NC
                pool.wait_ge(hhi_ready, count)
                g.tensor_tensor(h_lo[:, c, :], h32[:, c, :], h_hi[:, c, :], ALU.subtract).then_inc(hlo_ready, 1)

            for c in range(NC):
                pool.wait_ge(xhi_ready, c + 1)
                g.tensor_tensor(x_lo[:, c, :], x32[:, c, :], x_hi[:, c, :], ALU.subtract).then_inc(xlo_ready, 1)
            for c in range(AHEAD):
                state_news(c, c + 1)
                state_low(c, c + 1)
                state_news_low(c, c + 1)

            def slot(s0, off):
                low = off + (s0 if isinstance(s0, int) else LOOP_LO)

                def at(lag):
                    return s0 + (off - lag + 1)

                if has(low - 7) and has(low - 7 + NC):
                    c = (low - 7) % NC
                    pool.wait_ge(ghi_ready, at(7))
                    g.tensor_tensor(g_lo[:, c, :], g32[:, c, :], g_hi[:, c, :], ALU.subtract).then_inc(glo_ready, 1)
                if AHEAD <= low < NC:
                    state_news(low, low + 1)
                if has(low - 1) and low - 1 >= NC:
                    state_news(low - 1, at(1))
                if has(low - 4):
                    c, k = (low - 4) % NC, (low - 4) % 2
                    pool.wait_ge(gu_ready, at(4))
                    pool.wait_ge(score_ready, at(4))
                    g.tensor_tensor(gus[:, k, :], gu[:, k, :], score[:, c, :], ALU.mult).then_inc(gus_ready, 1)
                if AHEAD <= low < NC:
                    state_low(low, low + 1)
                    state_news_low(low, low + 1)
                if has(low - 1) and low - 1 >= NC:
                    state_news_low(low - 1, at(1))
                    state_low(low - 1, at(1))
                if has(low) and low >= NC:
                    c, k = low % NC, low % 2
                    pool.wait_ge(hc_ready, at(0))
                    g.tensor_tensor(d[:, k, :], h32[:, c, :], hc[:, k, :], ALU.subtract).then_inc(d_ready, 1)
                if has(low + 1) and low + 1 >= NC:
                    c = (low + 1) % NC
                    pool.wait_ge(xhi_ready, at(-1))
                    g.tensor_tensor(x_lo[:, c, :], x32[:, c, :], x_hi[:, c, :], ALU.subtract).then_inc(xlo_ready, 1)

            for s in range(0, LOOP_LO):
                slot(s - s % NC, s % NC)
            with pool.Fori(LOOP_LO, LOOP_HI, NC) as s0:
                for off in range(NC):
                    slot(s0, off)
            for s in range(LOOP_HI, LAST):
                slot(s - s % NC, s % NC)

        @block.scalar
        def _(act):
            a = nc.scalar
            act.wait_ge(zeroed, 1)
            a.activation(spare[:, :], ones[:, 0:1], ACT.Sigmoid)

            def reset_first(c):
                act.wait_ge(r_pe, c + 1)
                a.activation(r[:, c % 2, :], ps[:, B_R, :], ACT.Sigmoid, bias=b_zr[:, 1:2]).then_inc(r_ready, 1)

            def candidate_first(c):
                act.wait_ge(t2_ready, c + 1)
                a.activation(hc[:, c % 2, :], t[:, c % 2, :], ACT.Tanh, bias=b_h).then_inc(hc_ready, 1)

            def update_first(c):
                act.wait_ge(z_pe, c + 1)
                a.activation(ps[:, B_Z0[c % 2], :], ps[:, B_Z0[c % 2], :], ACT.Sigmoid, bias=b_zr[:, 0:1]).then_inc(z_ready, 1)

            def state_high(item, count):
                act.wait_ge(h_ready, count)
                a.activation(h_hi[:, item % NC, :], h32[:, item % NC, :], ACT.Copy).then_inc(hhi_ready, 1)

            def state_news_high(item, count):
                act.wait_ge(hn_ready, count)
                a.activation(hn_hi[:, item % 2, :], hn[:, item % 2, :], ACT.Copy).then_inc(hnhi_ready, 1)

            def news_part(c):
                act.wait_ge(news_pe, c + 1)
                a.activation(c_news[:, c, :], ps[:, B_NEWS[c], :], ACT.Identity,
                             bias=p_att[:, PACK_ATT["b1"]]).then_inc(c_ready, 1)

            for c in range(NC):
                act.wait_ge(x_landed[c], 16)
                a.activation(x_hi[:, c, :], x32[:, c, :], ACT.Copy).then_inc(xhi_ready, 1)
            act.wait_ge(b_ready, 1)
            reset_first(0)
            candidate_first(0)
            update_first(0)
            reset_first(1)
            state_high(0, 1)
            reset_first(2)
            candidate_first(1)
            state_news_high(0, 1)
            update_first(1)
            act.wait_ge(att_landed, 16)
            news_part(0)
            reset_first(3)
            candidate_first(2)
            update_first(2)
            state_high(1, 2)
            state_news_high(1, 2)
            news_part(1)
            candidate_first(3)
            update_first(3)
            news_part(2)

            def slot(s0, off):
                low = off + (s0 if isinstance(s0, int) else LOOP_LO)

                def at(lag):
                    return s0 + (off - lag + 1)

                def late(lag):
                    return s0 + (off - lag + 1 - NC)

                if has(low - 3):
                    act.wait_ge(a2_pe, at(3))
                    a.activation(a2l[:, (low - 3) % 2, :], ps[H:P, B_A2, :], ACT.Copy).then_inc(a2l_ready, 1)
                if has(low - 4):
                    act.wait_ge(score_pe, at(4))
                    a.activation(score[:, (low - 4) % NC, :], ps[:, B_SCORE, :], ACT.Sigmoid,
                                 bias=p_att[:, PACK_ATT["b3"]]).then_inc(score_ready, 1)
                    if low - 4 < NC:
                        act.wait_ge(gxh_pe, at(4))
                        a.activation(ps[:, B_GXH, :], ps[:, B_GXH, :], ACT.Tanh, bias=b_gated[:, 2:3]).then_inc(gc_ready, 1)
                    else:
                        act.wait_ge(gt2_ready, late(4))
                        a.activation(ps[:, B_GXH, :], gt[:, (low - 4) % 2, :], ACT.Tanh, bias=b_gated[:, 2:3]).then_inc(gc_ready, 1)
                if AHEAD <= low < NC:
                    state_high(low, low + 1)
                if has(low - 1) and low - 1 >= NC:
                    state_high(low - 1, at(1))
                if has(low) and low >= NC:
                    act.wait_ge(r_pe, at(0))
                    a.activation(r[:, low % 2, :], ps[:, B_R, :], ACT.Sigmoid, bias=b_zr[:, 1:2]).then_inc(r_ready, 1)
                if has(low - 2):
                    act.wait_ge(a1p_ready, at(2))
                    a.activation(a1_hi[:, (low - 2) % 2, :], ps[:, B_A1, :], ACT.Relu).then_inc(a1hi_ready, 1)
                if AHEAD <= low < NC:
                    state_news_high(low, low + 1)
                if has(low - 1) and low - 1 >= NC:
                    state_news_high(low - 1, at(1))
                if has(low - 3):
                    act.wait_ge(gu_pe, at(3))
                    a.activation(gu[:, (low - 3) % 2, :], ps[:, B_GU0 if low - 3 < NC else B_GU, :], ACT.Sigmoid, bias=b_gated[:, 0:1]).then_inc(gu_ready, 1)
                if has(low - 3):
                    act.wait_ge(a2p_ready, at(3))
                    a.activation(a2[0:H, (low - 3) % 2, :], ps[0:H, B_A2, :], ACT.Relu).then_inc(a2hi_ready, 1)
                if has(low + 3) and low + 3 >= NC:
                    c = (low + 3) % NC
                    act.wait_ge(x_landed[c], 4 * (s0 + (off + 3 - c)) + 16)
                    act.wait_ge(z_pe, at(1))
                    a.activation(x_hi[:, c, :], x32[:, c, :], ACT.Copy).then_inc(xhi_ready, 1)
                if has(low) and low >= NC:
                    k = low % 2
                    act.wait_ge(t2_ready, at(0))
                    a.activation(hc[:, k, :], t[:, k, :], ACT.Tanh, bias=b_h).then_inc(hc_ready, 1)
                if has(low - 6) and has(low - 6 + NC):
                    c = (low - 6) % NC
                    act.wait_ge(g_ready, at(6))
                    a.activation(g_hi[:, c, :], g32[:, c, :], ACT.Copy).then_inc(ghi_ready, 1)
                if has(low - 3) and low - 3 >= NC:
                    act.wait_ge(gr_pe, late(3))
                    a.activation(gr[:, (low - 3) % 2, :], ps[:, B_GR, :], ACT.Sigmoid, bias=b_gated[:, 1:2]).then_inc(gr_ready, 1)
                if has(low) and low >= NC:
                    act.wait_ge(z_pe, at(0))
                    a.activation(ps[:, B_Z, :], ps[:, B_Z, :], ACT.Sigmoid, bias=b_zr[:, 0:1]).then_inc(z_ready, 1)

            for s in range(0, LOOP_LO):
                slot(s - s % NC, s % NC)
                if s == 2:
                    news_part(3)
            with act.Fori(LOOP_LO, LOOP_HI, NC) as s0:
                for off in range(NC):
                    slot(s0, off)
            b_d1, b_d2 = p_rest[:, PACK_REST["b_d1"]], p_rest[:, PACK_REST["b_d2"]]
            b_f = p_rest[0:1, PACK_REST["b_f"]]
            for s in range(LOOP_HI, LAST):
                slot(s - s % NC, s % NC)

            def head_1(c):
                for k in range(2):
                    act.wait_ge(d1_pe, 2 * c + k + 1)
                    a.activation(y1p[:, c % 2, k, :], ps[:, B_D1[c][k], :], ACT.Identity,
                                 bias=b_d1[:, k:k + 1]).then_inc(y1p_ready, 1)

            def head_2(c):
                act.wait_ge(d2_pe, c + 1)
                a.activation(y2p[:, c % 2, :], ps[:, B_D2[c % 2], :], ACT.Identity, bias=b_d2).then_inc(y2p_ready, 1)

            def head_out(c):
                act.wait_ge(f_pe, c + 1)
                a.activation(y[0:1, c, :], ps[0:1, B_F[c % 2], :], ACT.Sigmoid, bias=b_f).then_inc(y_ready, 1)

            for c in range(NC + 3):
                if c < NC:
                    head_1(c)
                if 0 <= c - 1 < NC:
                    head_2(c - 1)
                if 0 <= c - 2 < NC:
                    head_out(c - 2)

        @block.vector
        def _(dve):
            v = nc.vector

            def split(k, lo, src):
                n = src.shape[1] // P
                hi_part = w_hi[:, lo:lo + n, :].rearrange("p k m -> p (k m)")
                lo_part = w_lo[:, lo:lo + n, :].rearrange("p k m -> p (k m)")
                v.tensor_copy(hi_part, src).then_inc(w_half, 1)
                dve.wait_ge(w_half, k + 1)
                v.tensor_tensor(lo_part, src, hi_part, ALU.subtract).then_inc(w_ready, 1)

            def prepare_att_terms():
                w3, w3_row = p_att[:, PACK_ATT["w3"]], p_att[:, PACK_ATT["w3_row"]]
                dve.wait_ge(att_landed, 16)
                v.tensor_tensor(w1_news[:, :], p_att[:, PACK_ATT["W1b"]], p_att[:, PACK_ATT["W1c"]], ALU.add).then_inc(prep, 1)
                v.tensor_tensor(w_att[:, 0, :], p_att[:, PACK_ATT["W1a"]], p_att[:, PACK_ATT["W1b"]], ALU.subtract).then_inc(prep, 1)
                v.tensor_copy(w_att[:, 1, :], p_att[:, PACK_ATT["W1d"]]).then_inc(prep, 1)
                v.scalar_tensor_tensor(out=w3_abs[:, :], in0=w3_row, scalar=-1.0, in1=w3_row,
                                       op0=ALU.mult, op1=ALU.max).then_inc(prep, 1)
                v.tensor_scalar(w3_col[:, 0:1], w3, 0.0, None, ALU.is_gt).then_inc(prep, 1)
                v.tensor_scalar(w3_col[:, 1:2], w3, 0.0, None, ALU.is_lt).then_inc(prep, 1)
                v.scalar_tensor_tensor(out=w3_col[:, 3:4], in0=w3, scalar=-1.0, in1=w3,
                                       op0=ALU.mult, op1=ALU.max).then_inc(prep, 1)

            def prepare_att_blocks():
                dve.wait_ge(prep, 7)
                v.tensor_tensor(w_att[:, 2, 0:H], p_att[:, PACK_ATT["W2"]], w3_abs[:, :], ALU.mult).then_inc(prep, 1)
                v.tensor_tensor(w_att[:, 2, H:P], p_att[:, PACK_ATT["W2"]], w3_abs[:, :], ALU.mult).then_inc(prep, 1)
                v.tensor_tensor(w3_col[:, 2:3], w3_col[:, 0:1], w3_col[:, 1:2], ALU.subtract).then_inc(prep, 1)
                v.tensor_tensor(b_att2[:, :], p_att[:, PACK_ATT["b2"]], w3_col[:, 3:4], ALU.mult).then_inc(prep, 1)
                dve.wait_ge(prep, 11)
                v.tensor_scalar(w3_sign[:, :], ones[:, :], w3_col[:, 2:3], None, ALU.mult).then_inc(prep, 1)

            def split_att():
                split(1, A_HS, w_att[:, :, :].rearrange("p k m -> p (k m)"))
                v.memset(w2_sum[:, 1, :], 0.0).then_inc(prep, 1)
                dve.wait_ge(prep, PREP_ATT)
                dve.wait_ge(w_ready, 2)
                v.tensor_copy(w2_sum[:, 0, 0:H], w_hi[:, A_2, 0:H]).then_inc(prep, 1)
                v.tensor_copy(w2_sum[:, 1, 0:H], w_hi[:, A_2, 0:H]).then_inc(prep, 1)
                v.tensor_copy(w2_sum[:, 0, H:P], w_lo[:, A_2, H:P]).then_inc(prep, 1)

            var, scale, shift, u, root = bn_t[:, 0, :], bn_t[:, 4, :], bn_t[:, 5, :], bn_t[:, 1, :], bn_t[:, 2, :]

            def bn_guess():
                dve.wait_ge(rest_landed, 16)
                v.tensor_scalar(var, p_rest[:, PACK_REST["var"]], BN_EPS, None, ALU.add).then_inc(bn_ready, 1)
                dve.wait_ge(bn_ready, 1)
                v.tensor_scalar(u.bitcast(I32), var.bitcast(I32), 1, None, ALU.logical_shift_right).then_inc(bn_ready, 1)
                dve.wait_ge(bn_ready, 2)
                v.tensor_scalar(root.bitcast(I32), u.bitcast(I32), -1, RSQRT_MAGIC, ALU.mult, ALU.add).then_inc(bn_ready, 1)

            def bn_newton(i):
                dve.wait_ge(bn_ready, 4 * i + 3)
                v.tensor_tensor(u, root, root, ALU.mult).then_inc(bn_ready, 1)
                dve.wait_ge(bn_ready, 4 * i + 4)
                v.tensor_tensor(u, u, var, ALU.mult).then_inc(bn_ready, 1)
                dve.wait_ge(bn_ready, 4 * i + 5)
                v.tensor_scalar(u, u, -0.5, 1.5, ALU.mult, ALU.add).then_inc(bn_ready, 1)
                dve.wait_ge(bn_ready, 4 * i + 6)
                v.tensor_tensor(root, root, u, ALU.mult).then_inc(bn_ready, 1)

            def bn_fold():
                dve.wait_ge(bn_ready, 4 * NEWTON + 3)
                v.tensor_tensor(scale, root, p_rest[:, PACK_REST["gamma"]], ALU.mult).then_inc(bn_ready, 1)
                dve.wait_ge(bn_ready, 4 * NEWTON + 4)
                v.tensor_tensor(u, p_rest[:, PACK_REST["mean"]], scale, ALU.mult).then_inc(bn_ready, 1)
                dve.wait_ge(bn_ready, 4 * NEWTON + 5)
                v.tensor_tensor(shift, p_rest[:, PACK_REST["beta"]], u, ALU.subtract).then_inc(bn_ready, 1)

            def bn_news():
                dve.wait_ge(bn_ready, 4 * NEWTON + 6)
                v.tensor_scalar(news_bn[:, :, :], news[:, :, :], scale[:, 1:2], shift[:, 1:2],
                                ALU.mult, ALU.add).then_inc(bn_ready, 1)

            def slot(s0, off):
                low = off + (s0 if isinstance(s0, int) else LOOP_LO)

                def at(lag):
                    return s0 + (off - lag + 1)

                def late(lag):
                    return s0 + (off - lag + 1 - NC)

                if has(low - 2):
                    if low - 2 < NC:
                        dve.wait_ge(c_ready, low - 1)
                    dve.wait_ge(a1_pe, at(2))
                    v.tensor_tensor(ps[:, B_A1, :], c_news[:, (low - 2) % NC, :], ps[:, B_A1, :], ALU.add).then_inc(a1p_ready, 1)
                if has(low - 3):
                    dve.wait_ge(a2l_ready, at(3))
                    v.scalar_tensor_tensor(out=ps[0:H, B_A2, :], in0=ps[0:H, B_A2, :], scalar=b_att2[0:H, 0:1],
                                           in1=a2l[:, (low - 3) % 2, :], op0=ALU.add, op1=ALU.add).then_inc(a2p_ready, 1)
                if has(low - 4):
                    dve.wait_ge(gc_ready, at(4))
                    v.tensor_tensor(ps[:, B_GXH, :], ps[:, B_GXH, :], g32[:, (low - 4) % NC, :], ALU.subtract).then_inc(gd_ready, 1)
                if has(low) and low >= NC:
                    k = low % 2
                    dve.wait_ge(hh_pe, late(0))
                    dve.wait_ge(r_ready, at(0))
                    v.scalar_tensor_tensor(out=t[:, k, :], in0=ps[:, B_HH, :], scalar=b_hs,
                                           in1=r[:, k, :], op0=ALU.add, op1=ALU.mult).then_inc(t1_ready, 1)
                if has(low - 4):
                    dve.wait_ge(gd_ready, at(4))
                    dve.wait_ge(gus_ready, at(4))
                    v.tensor_tensor(ps[:, B_GXH, :], ps[:, B_GXH, :], gus[:, (low - 4) % 2, :], ALU.mult).then_inc(ge_ready, 1)
                if has(low) and low >= NC:
                    k = low % 2
                    dve.wait_ge(t1_ready, at(0))
                    dve.wait_ge(xh_pe, at(0))
                    v.tensor_tensor(t[:, k, :], t[:, k, :], ps[:, B_XH, :], ALU.add).then_inc(t2_ready, 1)
                if has(low - 4):
                    c = (low - 4) % NC
                    dve.wait_ge(ge_ready, at(4))
                    v.tensor_tensor(g32[:, c, :], g32[:, c, :], ps[:, B_GXH, :], ALU.add).then_inc(g_ready, 1)
                if has(low - 2):
                    k = (low - 2) % 2
                    dve.wait_ge(a1hi_ready, at(2))
                    v.scalar_tensor_tensor(out=a1_lo[:, k, :], in0=ps[:, B_A1, :], scalar=0.0,
                                           in1=a1_hi[:, k, :], op0=ALU.max, op1=ALU.subtract).then_inc(a1lo_ready, 1)
                if has(low - 3):
                    k = (low - 3) % 2
                    dve.wait_ge(a2hi_ready, at(3))
                    v.scalar_tensor_tensor(out=a2[H:P, k, :], in0=ps[0:H, B_A2, :], scalar=0.0,
                                           in1=a2[0:H, k, :], op0=ALU.max, op1=ALU.subtract).then_inc(a2lo_ready, 1)
                if has(low - 3) and low - 3 >= NC:
                    k = (low - 3) % 2
                    dve.wait_ge(ghh_pe, late(3))
                    dve.wait_ge(gr_ready, late(3))
                    v.tensor_tensor(gt[:, k, :], gr[:, k, :], ps[:, B_GHH, :], ALU.mult).then_inc(gt1_ready, 1)
                if has(low) and low >= NC:
                    dve.wait_ge(d_ready, late(0))
                    dve.wait_ge(z_ready, at(0))
                    v.tensor_tensor(ps[:, B_Z, :], d[:, low % 2, :], ps[:, B_Z, :], ALU.mult).then_inc(e_ready, 1)
                if has(low - 3) and low - 3 >= NC:
                    k = (low - 3) % 2
                    dve.wait_ge(gxh_pe, at(3))
                    dve.wait_ge(gt1_ready, late(3))
                    v.tensor_tensor(gt[:, k, :], gt[:, k, :], ps[:, B_GXH, :], ALU.add).then_inc(gt2_ready, 1)
                if has(low) and low >= NC:
                    dve.wait_ge(e_ready, at(0))
                    v.tensor_tensor(h32[:, low % NC, :], hc[:, low % 2, :], ps[:, B_Z, :], ALU.add).then_inc(h_ready, 1)

            dve.wait_ge(gru_landed, 16)
            v.tensor_tensor(b_zr[:, :], gru_b[:, 0:2], gru_b[:, 3:5], ALU.add).then_inc(b_ready, 1)
            split(0, W_Z, p_gru[:, PACK_GRU["W"]])
            dve.wait_ge(zeroed, 2)

            def candidate_first(c):
                dve.wait_ge(r_ready, c + 1)
                v.tensor_scalar(t[:, c % 2, :], r[:, c % 2, :], b_hs, None, ALU.mult).then_inc(t1_ready, 1)
                dve.wait_ge(t1_ready, c + 1)
                dve.wait_ge(xh_pe, c + 1)
                v.tensor_tensor(t[:, c % 2, :], t[:, c % 2, :], ps[:, B_XH0[c % 2], :], ALU.add).then_inc(t2_ready, 1)

            def new_state_first(c):
                dve.wait_ge(hc_ready, c + 1)
                dve.wait_ge(z_ready, c + 1)
                v.tensor_tensor(ps[:, B_Z0[c % 2], :], hc[:, c % 2, :], ps[:, B_Z0[c % 2], :], ALU.mult).then_inc(e_ready, 1)
                dve.wait_ge(e_ready, c + 1)
                v.tensor_tensor(h32[:, c, :], hc[:, c % 2, :], ps[:, B_Z0[c % 2], :], ALU.subtract).then_inc(h_ready, 1)

            prepare_att_terms()
            candidate_first(0)
            prepare_att_blocks()
            new_state_first(0)
            candidate_first(1)
            split_att()
            candidate_first(2)
            new_state_first(1)
            candidate_first(3)
            dve.wait_ge(state_landed, 16)
            split(2, U_Z, p_state[:, :])
            new_state_first(2)
            for s in range(0, LOOP_LO):
                slot(s - s % NC, s % NC)
                if s == 2:
                    new_state_first(3)
                    dve.wait_ge(rest_landed, 16)
                    split(3, GW_U, p_rest[:, PACK_REST["gated"]])
                if s == NC:
                    bn_guess()
                if NC < s <= NC + NEWTON:
                    bn_newton(s - NC - 1)
                if s == NC + NEWTON + 1:
                    bn_fold()
                if s == NC + NEWTON + 2:
                    bn_news()
            with dve.Fori(LOOP_LO, LOOP_HI, NC) as s0:
                for off in range(NC):
                    slot(s0, off)
            for s in range(LOOP_HI, LAST):
                slot(s - s % NC, s % NC)
                if s >= ITEMS:
                    c = s - ITEMS
                    if c == 0:
                        dve.wait_ge(bn_ready, 4 * NEWTON + 7)
                    dve.wait_ge(g_ready, ITEMS - NC + c + 1)
                    v.tensor_scalar(g_bn[:, c, :], g32[:, c, :], bn_t[:, 4, 0:1], bn_t[:, 5, 0:1],
                                    ALU.mult, ALU.add).then_inc(gbn_ready, 1)

            def head_1(c):
                for k in range(2):
                    dve.wait_ge(y1p_ready, 2 * c + k + 1)
                    if c >= 2:
                        dve.wait_ge(d2_pe, c - 1)
                    v.scalar_tensor_tensor(out=y1[:, c % 2, k, :], in0=y1p[:, c % 2, k, :], scalar=LEAKY,
                                           in1=y1p[:, c % 2, k, :], op0=ALU.mult, op1=ALU.max).then_inc(y1_ready, 1)

            def head_2(c):
                dve.wait_ge(y2p_ready, c + 1)
                v.scalar_tensor_tensor(out=y2[:, c % 2, :], in0=y2p[:, c % 2, :], scalar=LEAKY,
                                       in1=y2p[:, c % 2, :], op0=ALU.mult, op1=ALU.max).then_inc(y2_ready, 1)

            for c in range(NC + 1):
                if c < NC:
                    head_1(c)
                if c >= 1:
                    head_2(c - 1)

        @block.tensor
        def _(pe):
            m = nc.tensor

            def split_product(bank, w, hi, lo, start, stop):
                m.matmul(ps[:, bank, :], w_hi[:, w, :], hi, start=start, stop=False)
                m.matmul(ps[:, bank, :], w_hi[:, w, :], lo, start=False, stop=False)
                return m.matmul(ps[:, bank, :], w_lo[:, w, :], hi, start=False, stop=stop)

            def news_part(c):
                if c == 0:
                    pe.wait_ge(news_landed, 16)
                    pe.wait_ge(prep, 1)
                if c == 2:
                    pe.wait_ge(c_ready, 1)
                if c == 3:
                    pe.wait_ge(t2_ready, 3)
                m.matmul(ps[:, B_NEWS[c], :], w1_news[:, :], news[:, c, :], start=True, stop=True).then_inc(news_pe, 1)

            pe.wait_ge(w_ready, 1)
            for c in range(NC):
                x = (x_hi[:, c, :], x_lo[:, c, :])
                pe.wait_ge(xlo_ready, c + 1)
                if c >= 1:
                    pe.wait_ge(r_ready, c)
                split_product(B_R, W_R, *x, start=True, stop=True).then_inc(r_pe, 1)
                if c >= 2:
                    pe.wait_ge(t2_ready, c - 1)
                split_product(B_XH0[c % 2], W_H, *x, start=True, stop=True).then_inc(xh_pe, 1)
                if c >= 2:
                    pe.wait_ge(h_ready, c - 1)
                split_product(B_Z0[c % 2], W_Z, *x, start=True, stop=True).then_inc(z_pe, 1)
                if c >= 1:
                    news_part(c - 1)

            def slot(s0, off):
                low = off + (s0 if isinstance(s0, int) else LOOP_LO)

                def at(lag):
                    return s0 + (off - lag + 1)

                def late(lag):
                    return s0 + (off - lag + 1 - NC)

                def parts(hi, lo, n, lag):
                    k = (low - lag) % n
                    return hi[:, k, :], lo[:, k, :]

                gru = has(low) and low >= NC
                gated = has(low - 3)
                state = gated and low - 3 >= NC
                x, h = parts(x_hi, x_lo, NC, 0), parts(h_hi, h_lo, NC, 0)
                h3, g3 = parts(h_hi, h_lo, NC, 3), parts(g_hi, g_lo, NC, 3)

                if has(low - 2):
                    if low == 2:
                        pe.wait_ge(w_ready, 2)
                    else:
                        pe.wait_ge(a1lo_ready, at(3))
                    pe.wait_ge(hlo_ready, at(2))
                    split_product(B_A1, A_HS, *parts(h_hi, h_lo, NC, 2), start=True, stop=False)
                    pe.wait_ge(hnlo_ready, at(2))
                    split_product(B_A1, A_HN, *parts(hn_hi, hn_lo, 2, 2), start=False, stop=True).then_inc(a1_pe, 1)
                if low == 2:
                    news_part(NC - 1)
                if gru:
                    if low - 4 < NC:
                        pe.wait_ge(r_ready, at(1))
                    else:
                        pe.wait_ge(gr_ready, late(4))
                    pe.wait_ge(xlo_ready, at(0))
                    split_product(B_R, W_R, *x, start=True, stop=False)
                    pe.wait_ge(hlo_ready, at(NC))
                    split_product(B_R, U_R, *h, start=False, stop=True).then_inc(r_pe, 1)
                if gated:
                    if low == 3:
                        pe.wait_ge(w_ready, 4)
                    if low == 3:
                        pe.wait_ge(h_ready, NC)
                    elif state and has(low - 1):
                        pe.wait_ge(h_ready, at(1))
                    else:
                        pe.wait_ge(gu_ready, at(4))
                    if not state:
                        split_product(B_GU0, GW_U, *h3, start=True, stop=True).then_inc(gu_pe, 1)
                    else:
                        split_product(B_GU, GW_U, *h3, start=True, stop=False)
                        pe.wait_ge(glo_ready, at(3 + NC))
                        split_product(B_GU, GU_U, *g3, start=False, stop=True).then_inc(gu_pe, 1)
                if gru:
                    pe.wait_ge(score_ready, at(4))
                    split_product(B_XH, W_H, *x, start=True, stop=True).then_inc(xh_pe, 1)
                if state:
                    if gru:
                        pe.wait_ge(r_ready, at(0))
                    else:
                        pe.wait_ge(gr_ready, late(4))
                    split_product(B_GR, GW_R, *h3, start=True, stop=False)
                    split_product(B_GR, GU_R, *g3, start=False, stop=True).then_inc(gr_pe, 1)
                    if low - 3 > NC:
                        pe.wait_ge(gt1_ready, late(4))
                    else:
                        pe.wait_ge(gu_ready, NC)
                    split_product(B_GHH, GU_C, *g3, start=True, stop=True).then_inc(ghh_pe, 1)
                if gru:
                    if state:
                        pe.wait_ge(gu_ready, at(3))
                    else:
                        pe.wait_ge(h_ready, at(1))
                    split_product(B_Z, W_Z, *x, start=True, stop=False)
                    split_product(B_Z, U_Z, *h, start=False, stop=True).then_inc(z_pe, 1)
                if low in (ITEMS, ITEMS + 2):
                    head_1_news(0, (low - ITEMS) // 2)
                if gated:
                    if low > 3:
                        pe.wait_ge(g_ready, at(4))
                    else:
                        pe.wait_ge(c_ready, 3)
                    split_product(B_GXH, GW_C, *h3, start=True, stop=True).then_inc(gxh_pe, 1)
                if has(low - 2):
                    a1 = parts(a1_hi, a1_lo, 2, 2)
                    if low == 2:
                        pe.wait_ge(c_ready, 2)
                        pe.wait_ge(prep, PREP_ATT + 3)
                    else:
                        pe.wait_ge(a2lo_ready, at(3))
                    pe.wait_ge(a1lo_ready, at(2))
                    m.matmul(ps[:, B_A2, :], w2_sum[:, 0, :], a1[0], start=True, stop=False)
                    m.matmul(ps[:, B_A2, :], w2_sum[:, 1, :], a1[1], start=False, stop=True).then_inc(a2_pe, 1)
                if gated:
                    if low == 3:
                        pe.wait_ge(c_ready, NC)
                    elif has(low):
                        pe.wait_ge(t2_ready, at(0))
                    else:
                        pe.wait_ge(score_ready, at(4))
                    pe.wait_ge(a2lo_ready, at(3))
                    m.matmul(ps[:, B_SCORE, :], w3_sign[:, :], a2[:, (low - 3) % 2, :], start=True, stop=True).then_inc(score_pe, 1)
                if has(low + 1) and low + 1 >= NC:
                    if low + 1 == NC:
                        pe.wait_ge(w_ready, 3)
                        pe.wait_ge(t2_ready, NC)
                    else:
                        pe.wait_ge(t1_ready, at(0))
                    pe.wait_ge(hlo_ready, at(NC - 1))
                    split_product(B_HH, U_H, *parts(h_hi, h_lo, NC, -1), start=True, stop=True).then_inc(hh_pe, 1)

            for s in range(0, LOOP_LO):
                slot(s - s % NC, s % NC)
            with pe.Fori(LOOP_LO, LOOP_HI, NC) as s0:
                for off in range(NC):
                    slot(s0, off)
            def head_1_news(c, k):
                if c == 0 and k == 0:
                    pe.wait_ge(bn_ready, 4 * NEWTON + 7)
                    pe.wait_ge(t1_ready, ITEMS)
                if c == 0 and k == 1:
                    pe.wait_ge(a1lo_ready, ITEMS)
                if c == 1:
                    pe.wait_ge((gr_ready, a2lo_ready)[k], (ITEMS - NC, ITEMS)[k])
                if c == 2:
                    pe.wait_ge((gu_ready, gt1_ready)[k], (ITEMS, ITEMS - NC)[k])
                if c == 3:
                    pe.wait_ge(y1p_ready, k + 1)
                m.matmul(ps[:, B_D1[c][k], :], dw1[:, 1, k * P:(k + 1) * P], news_bn[:, c, :], start=True, stop=False)

            def head_1_state(c):
                pe.wait_ge(gbn_ready, c + 1)
                for k in range(2):
                    m.matmul(ps[:, B_D1[c][k], :], dw1[:, 0, k * P:(k + 1) * P], g_bn[:, c, :],
                             start=False, stop=True).then_inc(d1_pe, 1)

            def head_2(c):
                if c < 2:
                    pe.wait_ge((score_ready, g_ready)[c], ITEMS)
                else:
                    pe.wait_ge(y2p_ready, c - 1)
                bank = B_D2[c % 2]
                pe.wait_ge(y1_ready, 2 * c + 2)
                m.matmul(ps[:, bank, :], dw2[:, 0, :], y1[:, c % 2, 0, :], start=True, stop=False)
                m.matmul(ps[:, bank, :], dw2[:, 1, :], y1[:, c % 2, 1, :], start=False, stop=True).then_inc(d2_pe, 1)

            def head_out(c):
                if c < 2:
                    pe.wait_ge(y1p_ready, 4)
                else:
                    pe.wait_ge(y_ready, c - 1)
                pe.wait_ge(y2_ready, c + 1)
                m.matmul(ps[0:1, B_F[c % 2], :], p_rest[:, PACK_REST["F"]], y2[:, c % 2, :],
                         start=True, stop=True).then_inc(f_pe, 1)

            for s in range(LOOP_HI, LAST):
                slot(s - s % NC, s % NC)
            head_1_state(0)
            for c in range(1, NC + 3):
                if c < NC:
                    head_1_news(c, 0)
                    head_1_news(c, 1)
                    head_1_state(c)
                if 0 <= c - 1 < NC:
                    head_2(c - 1)
                if 0 <= c - 2 < NC:
                    head_out(c - 2)


def kernel(**inputs):
    import numpy as np
    import concourse.bacc as bacc
    from concourse.bass_utils import run_bass_kernel_spmd

    w = {k[len("L0_rec_"):]: np.asarray(v) for k, v in inputs.items() if k != "r_inputs"}
    x = np.asarray(inputs["r_inputs"])

    def column(v):
        return v.reshape(-1, P).T

    def row(v):
        return np.broadcast_to(v.reshape(1, -1), (P, v.size))

    def twice(v):
        return np.concatenate([v.reshape(H, 1)] * 2)

    def pack(parts, n):
        out = np.ascontiguousarray(np.concatenate(parts, axis=1))
        assert out.shape == (P, n)
        return out

    w1 = w["att_W1"]
    arrays = {
        "xs": np.ascontiguousarray(x.transpose(1, 2, 0)),
        "pack_gru": pack([w["gru_W"], column(w["gru_b"])], N_GRU),
        "pack_state": pack([w["gru_U"]], N_STATE),
        "pack_att": pack([w1[0:P], w1[P:2 * P], w1[2 * P:3 * P], w1[3 * P:4 * P], w["att_W2"], row(w["att_W3"]),
                          twice(w["att_W3"]), column(w["att_b1"]), twice(w["att_b2"]), row(w["att_b3"])], N_ATT),
        "pack_rest": pack([w["au_Wu"], w["au_Wr"], w["au_Wc"], w["au_Uu"], w["au_Ur"], w["au_Uc"],
                           column(w["au_bu"]), column(w["au_br"]), column(w["au_bc"]),
                           column(w["bn_gamma"]), column(w["bn_beta"]), column(w["bn_mean"]), column(w["bn_var"]),
                           w["d_W1"][0:P], w["d_W1"][P:2 * P], w["d_W2"][0:P], w["d_W2"][P:2 * P], w["f_W"],
                           column(w["d_b1"]), column(w["d_b2"]), row(w["f_b"])], N_REST),
    }
    nc = bacc.Bacc("TRN2", target_bir_lowering=False, num_devices=1)
    feed, args = {}, []
    for name, value in arrays.items():
        feed[f"in_{name}"] = value
        args.append(nc.dram_tensor(f"in_{name}", value.shape, mybir.dt.from_np(value.dtype), kind="ExternalInput").ap())
    out = nc.dram_tensor("out_y", (1, x.shape[0]), F32, kind="ExternalOutput").ap()
    rec_kernel(nc, *args, out)
    result = run_bass_kernel_spmd(nc, [feed], core_ids=[0])
    return result.results[0]["out_y"].reshape(x.shape[0], 1)
```
